# Optimizing a Trainium2 kernel written in Bass

```python
import numpy as np
import jax
import jax.numpy as jnp

def _softmax(x, axis=-1):
    return jax.nn.softmax(x, axis=axis)

def _gelu(x):
    return jax.nn.gelu(x, approximate=True)

def _silu(x):
    return jax.nn.silu(x)

def _sigmoid(x):
    return jax.nn.sigmoid(x)

def _layernorm(x, axis=-1, eps=1e-05):
    m = jnp.mean(x, axis=axis, keepdims=True)
    v = jnp.var(x, axis=axis, keepdims=True)
    return (x - m) / jnp.sqrt(v + eps)

def _scatter_add(tgt, idx, src, axis=0):
    return tgt.at[idx].add(src)

def _segment_sum(src, seg, n):
    return jax.ops.segment_sum(src, seg, n)
kernel_name = 'mk_perceiver_d1_seqx_r8_48fa9b'

def setup_inputs(seed: int=0):
    np.random.seed(seed)
    _w = jnp.asarray

    def _rec_inputs():
        import jax
        import jax.numpy as jnp
        _rk = jax.random.key(seed)
        x = -0.000125 + 0.9999 * jax.random.normal(jax.random.fold_in(_rk, 1), (1, 128, 256), jnp.float32)
        _lenS = 128 - jax.random.randint(jax.random.fold_in(_rk, 7), (1,), 0, max(1, 128 // 4) + 1, jnp.int32)
        _lenS2 = 2048 - jax.random.randint(jax.random.fold_in(_rk, 8), (1,), 0, max(1, 2048 // 4) + 1, jnp.int32)
        _ctx_2048P = jax.random.normal(jax.random.fold_in(_rk, 11), (1, 16, 256), jnp.float32)
        _ctx_2048c = jax.random.dirichlet(jax.random.fold_in(_rk, 511), 0.3 * jnp.ones((16,), jnp.float32), (1, 2048))
        _ctx_2048t = jnp.einsum('bsk,bkd->bsd', _ctx_2048c, _ctx_2048P)
        _ctx_2048t = _ctx_2048t * jax.lax.rsqrt(jnp.mean(jnp.square(_ctx_2048t)) + 1e-12) * 0.953939
        ctx_2048 = -0.000514642 + 1.00011 * (_ctx_2048t + 0.3 * jax.random.normal(jax.random.fold_in(_rk, 611), (1, 2048, 256), jnp.float32))
        _validS = jnp.arange(128)[None, :] < _lenS[:, None]
        _validS2 = jnp.arange(2048)[None, :] < _lenS2[:, None]
        _causal = jnp.tril(jnp.ones((128, 128), dtype=bool))
        mask_BxS2_bk0 = jnp.logical_not(jnp.broadcast_to(_validS2[:, :], (1, 2048)))
        return (x, ctx_2048, mask_BxS2_bk0)
    x, ctx_2048, mask_BxS2_bk0 = _rec_inputs()

    def _L0_xattn_setup():
        import jax, jax.numpy as jnp
        import numpy as np
        H = 256
        NH = 16
        HD = H // NH
        EPS = 1e-06

        def rmsnorm(x, w, eps=EPS):
            var = jnp.mean(x * x, axis=-1, keepdims=True)
            return x * jax.lax.rsqrt(var + eps) * w
        key = jax.random.key(seed)
        ks = jax.random.split(key, 9)
        B, L, M = (4, 512, 32)
        s = 1.0 / np.sqrt(H)
        return {'hidden_states': jax.random.normal(ks[0], (B, L, H), dtype=jnp.float32), 'memory_tokens': jax.random.normal(ks[1], (B, M, H), dtype=jnp.float32), 'memory_mask': jax.random.randint(ks[2], (B, M), 0, 2).astype(bool), 'norm_w': jnp.ones((H,), dtype=jnp.float32), 'wq': jax.random.normal(ks[3], (H, H), dtype=jnp.float32) * s, 'wk': jax.random.normal(ks[4], (H, H), dtype=jnp.float32) * s, 'wv': jax.random.normal(ks[5], (H, H), dtype=jnp.float32) * s, 'wo': jax.random.normal(ks[6], (H, H), dtype=jnp.float32) * s, 'wg': jax.random.normal(ks[7], (H, H), dtype=jnp.float32) * s}
    _L0_xattn_all = _L0_xattn_setup()
    _L0_xattn_in = {k: v for k, v in _L0_xattn_all.items() if k in ('norm_w', 'wq', 'wk', 'wv', 'wo', 'wg')}
    del _L0_xattn_all

    def _L0_attn_setup():
        import jax, jax.numpy as jnp
        import numpy as np
        DIM = 256
        H = 16
        D = DIM // H // 2
        LAYER_NUM = 12
        LAM_INIT = 0.8 - 0.6 * float(np.exp(-0.3 * LAYER_NUM))
        SCALE = D ** (-0.5)
        EPS = 1e-05

        def _split_qk(y, b, n):
            y = y.reshape(b, n, H, D, 2)
            y = y.transpose(0, 1, 4, 2, 3)
            return y.reshape(b, n, 2 * H, D)
        key = jax.random.key(seed)
        ks = jax.random.split(key, 10)
        B, N = (4, 512)
        return {'x': jax.random.normal(ks[0], (B, N, DIM), dtype=jnp.float32), 'Wq': jax.random.normal(ks[1], (DIM, DIM), dtype=jnp.float32) * DIM ** (-0.5), 'Wk': jax.random.normal(ks[2], (DIM, DIM), dtype=jnp.float32) * DIM ** (-0.5), 'Wv': jax.random.normal(ks[3], (DIM, DIM), dtype=jnp.float32) * DIM ** (-0.5), 'Wo': jax.random.normal(ks[4], (DIM, DIM), dtype=jnp.float32) * DIM ** (-0.5), 'bo': jax.random.normal(ks[5], (DIM,), dtype=jnp.float32) * 0.01, 'lq1': jax.random.normal(ks[6], (D,), dtype=jnp.float32) * 0.1, 'lq2': jax.random.normal(ks[7], (D,), dtype=jnp.float32) * 0.1, 'lk1': jax.random.normal(ks[8], (D,), dtype=jnp.float32) * 0.1, 'lk2': jax.random.normal(ks[9], (D,), dtype=jnp.float32) * 0.1}
    _L0_attn_all = _L0_attn_setup()
    _L0_attn_in = {k: v for k, v in _L0_attn_all.items() if k in ('Wq', 'Wk', 'Wv', 'Wo', 'bo', 'lq1', 'lq2', 'lk1', 'lk2')}
    del _L0_attn_all

    def _L0_ffn_setup():
        import jax, jax.numpy as jnp
        import numpy as np
        B, S, H, I, E, K = (4, 256, 256, 512, 8, 2)
        key = jax.random.key(seed)
        k1, k2, k3, k4 = jax.random.split(key, 4)
        return {'hidden_states': jax.random.normal(k1, (B, S, H), dtype=jnp.float32), 'gate_weight': jax.random.normal(k2, (E, H), dtype=jnp.float32) * 0.02, 'gate_up_proj': jax.random.normal(k3, (E, 2 * I, H), dtype=jnp.float32) * 0.02, 'down_proj': jax.random.normal(k4, (E, H, I), dtype=jnp.float32) * 0.02}
    _L0_ffn_all = _L0_ffn_setup()
    _L0_ffn_in = {k: v for k, v in _L0_ffn_all.items() if k in ('gate_weight', 'gate_up_proj', 'down_proj')}
    del _L0_ffn_all
    return {'x': x, 'ctx_2048': ctx_2048, 'mask_BxS2_bk0': mask_BxS2_bk0, 'L0_xattn_norm_w': _L0_xattn_in['norm_w'], 'L0_xattn_wq': _L0_xattn_in['wq'], 'L0_xattn_wk': _L0_xattn_in['wk'], 'L0_xattn_wv': _L0_xattn_in['wv'], 'L0_xattn_wo': _L0_xattn_in['wo'], 'L0_xattn_wg': _L0_xattn_in['wg'], 'L0_attn_Wq': _L0_attn_in['Wq'], 'L0_attn_Wk': _L0_attn_in['Wk'], 'L0_attn_Wv': _L0_attn_in['Wv'], 'L0_attn_Wo': _L0_attn_in['Wo'], 'L0_attn_bo': _L0_attn_in['bo'], 'L0_attn_lq1': _L0_attn_in['lq1'], 'L0_attn_lq2': _L0_attn_in['lq2'], 'L0_attn_lk1': _L0_attn_in['lk1'], 'L0_attn_lk2': _L0_attn_in['lk2'], 'L0_ffn_gate_weight': _L0_ffn_in['gate_weight'], 'L0_ffn_gate_up_proj': _L0_ffn_in['gate_up_proj'], 'L0_ffn_down_proj': _L0_ffn_in['down_proj']}

def reference(x, ctx_2048, mask_BxS2_bk0, L0_xattn_norm_w, L0_xattn_wq, L0_xattn_wk, L0_xattn_wv, L0_xattn_wo, L0_xattn_wg, L0_attn_Wq, L0_attn_Wk, L0_attn_Wv, L0_attn_Wo, L0_attn_bo, L0_attn_lq1, L0_attn_lq2, L0_attn_lk1, L0_attn_lk2, L0_ffn_gate_weight, L0_ffn_gate_up_proj, L0_ffn_down_proj):
    import jax
    import jax.numpy as jnp

    def _L0_xattn_ref(hidden_states, memory_tokens, memory_mask, norm_w, wq, wk, wv, wo, wg):
        import jax, jax.numpy as jnp
        import numpy as np
        H = 256
        NH = 16
        HD = H // NH
        EPS = 1e-06

        def rmsnorm(x, w, eps=EPS):
            var = jnp.mean(x * x, axis=-1, keepdims=True)
            return x * jax.lax.rsqrt(var + eps) * w
        B, L, C = hidden_states.shape
        M = memory_tokens.shape[1]
        scale = HD ** (-0.5)
        x = rmsnorm(hidden_states, norm_w)
        q = (x @ wq.T).reshape(B, L, NH, HD)
        k = (memory_tokens @ wk.T).reshape(B, M, NH, HD)
        v = (memory_tokens @ wv.T).reshape(B, M, NH, HD)
        attn = jnp.einsum('blhd,bmhd->bhlm', q, k) * scale
        attn = jnp.where(memory_mask[:, None, None, :], attn, -jnp.inf)
        attn = jax.nn.softmax(attn, axis=-1)
        attn = jnp.nan_to_num(attn, nan=0.0)
        out = jnp.einsum('bhlm,bmhd->blhd', attn, v).reshape(B, L, C)
        out = out @ wo.T
        gate = jax.nn.sigmoid(x @ wg.T)
        return gate * out

    def _L0_attn_ref(x, Wq, Wk, Wv, Wo, bo, lq1, lq2, lk1, lk2):
        import jax, jax.numpy as jnp
        import numpy as np
        DIM = 256
        H = 16
        D = DIM // H // 2
        LAYER_NUM = 12
        LAM_INIT = 0.8 - 0.6 * float(np.exp(-0.3 * LAYER_NUM))
        SCALE = D ** (-0.5)
        EPS = 1e-05

        def _split_qk(y, b, n):
            y = y.reshape(b, n, H, D, 2)
            y = y.transpose(0, 1, 4, 2, 3)
            return y.reshape(b, n, 2 * H, D)
        b, n, _ = x.shape
        q = _split_qk(x @ Wq.T, b, n) * SCALE
        k = _split_qk(x @ Wk.T, b, n)
        v = (x @ Wv.T).reshape(b, n, H, 2 * D).transpose(0, 2, 1, 3)
        att = jnp.einsum('bnqd,bnkd->bnqk', q, k)
        att = jnp.nan_to_num(att)
        att = jax.nn.softmax(att.astype(jnp.float32), axis=-1)
        lam = jnp.exp(jnp.sum(lq1 * lk1)) - jnp.exp(jnp.sum(lq2 * lk2)) + LAM_INIT
        diff = att[:, :, :H, :H] - lam * att[:, :, H:, H:]
        out = jnp.einsum('bnah,bhnd->bnad', diff, v)
        out = out * jax.lax.rsqrt(jnp.mean(out * out, axis=-1, keepdims=True) + EPS)
        out = out * (1.0 - LAM_INIT)
        out = out.reshape(b, n, DIM)
        return out @ Wo.T + bo

    def _L0_ffn_ref(hidden_states, gate_weight, gate_up_proj, down_proj):
        import jax, jax.numpy as jnp
        import numpy as np
        B, S, H, I, E, K = (4, 256, 256, 512, 8, 2)
        b, s, h = hidden_states.shape
        num_experts, top_k = (gate_weight.shape[0], K)
        x = hidden_states.reshape(-1, h)
        router_logits = x @ gate_weight.T
        probs = jax.nn.softmax(router_logits.astype(jnp.float32), axis=-1)
        top_v, top_i = jax.lax.top_k(probs, top_k)
        top_v = top_v / top_v.sum(axis=-1, keepdims=True)
        combine_w = jnp.einsum('tke,tk->te', jax.nn.one_hot(top_i, num_experts, dtype=top_v.dtype), top_v).astype(x.dtype)

        def expert_step(acc, inp):
            gu, dp, w = inp
            gate, up = jnp.split(x @ gu.T, 2, axis=-1)
            hidden = jax.nn.silu(gate) * up
            y = hidden @ dp.T
            return (acc + w[:, None] * y, None)
        out, _ = jax.lax.scan(expert_step, jnp.zeros_like(x), (gate_up_proj, down_proj, combine_w.T))
        return out.reshape(b, s, h)
    x = x + _L0_xattn_ref(_layernorm(x, axis=-1), ctx_2048, mask_BxS2_bk0, L0_xattn_norm_w, L0_xattn_wq, L0_xattn_wk, L0_xattn_wv, L0_xattn_wo, L0_xattn_wg)
    x = x + _L0_attn_ref(_layernorm(x, axis=-1), L0_attn_Wq, L0_attn_Wk, L0_attn_Wv, L0_attn_Wo, L0_attn_bo, L0_attn_lq1, L0_attn_lq2, L0_attn_lk1, L0_attn_lk2)
    x = x + _L0_ffn_ref(_layernorm(x, axis=-1), L0_ffn_gate_weight, L0_ffn_gate_up_proj, L0_ffn_down_proj)
    return x

_drawn_inputs = setup_inputs


def setup_inputs(seed=0):
    import zlib

    import numpy as np

    out = dict(_drawn_inputs(seed))
    spreads = {'L0_xattn_norm_w': (1.0, 0.2)}
    factors = {'L0_attn_bo': 5.74,
     'L0_attn_lq1': 8.0,
     'L0_attn_lq2': 7.4,
     'L0_attn_lk1': 4.874,
     'L0_attn_lk2': 8.0,
     'L0_ffn_gate_weight': 3.901,
     'L0_ffn_gate_up_proj': 3.436,
     'L0_ffn_down_proj': 3.469}
    for name, (base, spread) in spreads.items():
        noise = np.random.default_rng([zlib.crc32(name.encode()), seed]).standard_normal(out[name].shape)
        drawn = base * np.exp(spread * noise) if base else spread * noise
        out[name] = jnp.asarray(drawn.astype(out[name].dtype))
    for name, factor in factors.items():
        out[name] = (out[name] * factor).astype(out[name].dtype)
    return out
```

```python
from contextlib import ExitStack

import numpy as np

import concourse.bass as bass
from concourse import mybir

F32 = mybir.dt.float32
F32R = mybir.dt.float32r
U8 = mybir.dt.uint8
ALU = mybir.AluOpType
ACT = mybir.ActivationFunctionType
AX = mybir.AxisListType

P = 128
T = 128
C = 256
KC = C // P
S = 2048
NH, HD = 16, 16
PAIRS = NH // 2
ROWS = 2 * HD * 3
ONES_ROW, MASK_ROW = ROWS, ROWS + 1
KROWS = ROWS + 2
BANK = 512
KCH = S // BANK
KB = S // P
HALF = 2 * BANK
NPIECE = NH * S // HALF
CHUNKS = PAIRS * KB // 2
PT = 4
VW = 32
D2 = HD // 2
SUB = 2 * NH
E, I = 8, 512
IC = I // P
MASKED = -float(2.0 ** 100)
FLOOR = -float(2.0 ** 96)
FMAX = 3.4028234663852886e38
LAM_INIT = 0.8 - 0.6 * float(np.exp(-0.3 * 12))
LN_EPS, RMS_EPS = 1e-5, 1e-6

C_M0, C_M1, C_S0, C_S1, C_KS, C_KB, C_PW = range(7)
C_ID = 8
C_NEG = C_ID + P
C_SEL = C_NEG + P
C_TRI = C_SEL + 64
C_ALL = C_TRI + E * E


def constants():
    c = np.zeros((P, C_ALL), np.float32)
    r = np.arange(ROWS)
    scale = HD ** -0.5
    for j in range(2):
        own = (r // (ROWS // 2)) == j
        c[:ROWS, C_M0 + j] = own * scale
        c[:ROWS, C_S0 + j] = (own & (r % 3 == 1)) * -scale
    c[ONES_ROW, C_KS], c[ONES_ROW, C_KB] = 0.0, 1.0
    c[MASK_ROW, C_KS], c[MASK_ROW, C_KB] = -MASKED, MASKED
    c[:, C_PW] = -0.5
    c[:, C_ID:C_ID + P] = np.eye(P)
    c[:, C_NEG:C_NEG + P] = -np.eye(P)
    q = np.arange(P)
    c[q, C_SEL + 32 * (q // 64) + q % 32] = 1.0
    c[:, C_TRI:C_TRI + E * E] = np.tril(np.ones((E, E)), -1).reshape(-1)
    return c


def perceiver_layer(nc, x, ctxT, mask2, cst, norm_w, wk, wv, wqs, wg, wo, wqkv, wo2, bo, lams, wr, wgu, wdn, out):
    with ExitStack() as ctx:
        def sb(name, shape, dt=F32):
            return ctx.enter_context(nc.sbuf_tensor(name, shape, dt))

        def sem(name):
            return ctx.enter_context(nc.semaphore(name))

        base = (nc.sbuf_base + 63) // 64 * 64
        KIB = 1024
        arena = sb("arena", [P, 144 * KIB // 4 + 16])

        def at(name, shape, kib, dt=F32):
            return nc.alloc_sbuf_tensor_at(name, shape, dt, offset=base + kib * KIB)

        kstack = [at("kstack_a", [P, 4, S], 0, F32R), at("kstack_b", [P, 4, S], 32, F32R)]
        ctx_hi = at("ctx_hi", [P, KC, S], 32, F32R)
        ctx_lo = at("ctx_lo", [P, KC, S], 48, F32R)
        vals = at("vals", [P, KB, NH, VW], 64)
        ctx_raw = at("ctx_raw", [P, KC, S], 64)
        k_hi = at("k_hi", [P, 2, S], 96, F32R)
        k_lo = at("k_lo", [P, 2, S], 112, F32R)
        probs = at("probs", [P, PT, BANK], 128)
        qneg = at("qneg", [KROWS, 2, PAIRS, T], 128, F32R)
        qstack = at("qstack", [P, PAIRS, 2, T], 136, F32R)
        w_at = [96, 108, 0, 12, 32, 44, 64, 76]
        gu_w = [at(f"gate_up{e}", [P, KC, 2 * I], w_at[e]) for e in range(E)]
        dn_w = [at(f"down{e}", [P, IC, C], w_at[e] + 8) for e in range(E)]
        prod = [at(f"prod{i}", [P, 1024], kib) for i, kib in enumerate([24, 28, 56, 60, 88, 92, 120, 124])]
        shifted = at("shifted", [P, SUB, SUB], 128)
        th, hT = at("th", [P, 2, I], 24), at("hT", [P, 2, I], 28)

        cs = sb("cs", [P, C_ALL])
        ident, nident = cs[:, C_ID:C_ID + P], cs[:, C_NEG:C_NEG + P]
        nw = sb("nw", [P, KC])
        xs = sb("xs", [P, C])
        mask_u8 = sb("mask_u8", [P, S], U8)
        wk_s, wk_hi, wk_lo = sb("wk_s", [P, KC, C]), sb("wk_hi", [P, KC, C], F32R), sb("wk_lo", [P, KC, C], F32R)
        wv_s, wv_hi, wv_lo = sb("wv_s", [P, KC, C]), sb("wv_hi", [P, KC, C], F32R), sb("wv_lo", [P, KC, C], F32R)
        wq_s = sb("wq_s", [P, KC, PAIRS, KROWS])
        wg_s, wo_s, wo2_s = sb("wg_s", [P, KC, C]), sb("wo_s", [P, KC, C]), sb("wo2_s", [P, KC, C])
        wqkv_s = sb("wqkv_s", [P, KC, 3 * C])
        bo_s, lam_s, wr_s = sb("bo_s", [P, C]), sb("lam_s", [P, 4, D2]), sb("wr_s", [P, KC, E])
        stat, mv, rstd, ms = sb("stat", [P, 3, 6]), sb("mv", [P, 3, 2]), sb("rstd", [P, 3]), sb("ms", [P, 2])
        junk, hn, h2 = sb("junk", [P, C]), sb("hn", [P, C]), sb("h2", [P, C])
        xnT = sb("xnT", [P, KC, T])
        gate = sb("gate", [P, C])
        part_max, row_max = sb("part_max", [P, NPIECE]), sb("row_max", [P, NH])
        acc_s = sb("acc_s", [P, PAIRS, T])
        den, rden = sb("den", [P, NH]), sb("rden", [P, NH])
        o1, oT = sb("o1", [P, NH, HD]), sb("oT", [P, KC, T])
        x1, x1b, x1n, x1T = sb("x1", [P, C]), sb("x1b", [P, C]), sb("x1n", [P, C]), sb("x1T", [P, KC, T])
        qd, kd, vd = sb("qd", [P, D2, SUB]), sb("kd", [P, D2, SUB]), sb("vd", [P, NH, HD])
        smax, ssum, srec = sb("smax", [P, SUB]), sb("ssum", [P, SUB]), sb("srec", [P, SUB])
        dif, dif1 = sb("dif", [P, NH, NH]), sb("dif1", [P, NH, NH])
        lsum, lexp, nlam = sb("lsum", [P, 2]), sb("lexp", [P, 2]), sb("nlam", [P, 1])
        sq, ssq, rms = sb("sq", [P, NH, HD]), sb("ssq", [P, NH]), sb("rms", [P, NH])
        x2, x2n, x2T = sb("x2", [P, C]), sb("x2n", [P, C]), sb("x2T", [P, KC, T])
        lg, rk, rk2 = sb("lg", [P, E]), sb("rk", [P, E, E]), sb("rk2", [P, E, E])
        rank, lmax, lex, wsel, wsum = sb("rank", [P, E]), sb("lmax", [P, 1]), sb("lex", [P, E]), sb("wsel", [P, E]), sb("wsum", [P, 2])

        ps = ctx.enter_context(nc.psum_tensor("ps", [P, 8, BANK], F32))
        scratch = nc.dram_tensor("k_parts", [2 * P, 3, S], F32)

        ld = {n: sem("loaded_" + n) for n in
              ("x", "cst", "wk", "wv", "wq", "wg", "nw", "mask", "wo", "wqkv", "wo2", "small")}
        ld_ctx = [sem(f"loaded_ctx{i}") for i in range(KCH)]
        ld_exp = [sem(f"loaded_expert{e}") for e in range(E)]
        k_saved = [sem(f"k_saved{m}") for m in range(2)]
        kst_loaded = [sem(f"kstack_loaded{p}") for p in range(PAIRS)]
        out_saved = sem("out_saved")
        vchain, achain, pchain = sem("vector_chain"), sem("scalar_chain"), sem("pool_chain")
        wk_split, wv_split = sem("wk_split"), sem("wv_split")
        ctx_hi_done, ctx_lo_done = sem("ctx_hi_done"), sem("ctx_lo_done")
        kproj, k_hi_done, k_lo_done = sem("k_projected"), sem("k_hi_done"), sem("k_lo_done")
        vproj, v_even, v_odd = sem("v_projected"), sem("v_kept_even"), sem("v_kept_odd")
        v_pads = sem("v_pads")
        kst_const = sem("kstack_constant_rows")
        var_ready, rstd_ready = sem("variance_ready"), sem("rstd_ready")
        xn_ready, xT_ready, xT_kept = sem("xn_ready"), sem("xT_ready"), sem("xT_kept")
        qproj, q_kept, q_rows = sem("q_projected"), sem("q_kept"), sem("q_constant_rows")
        gproj, g_kept = sem("gate_projected"), sem("gate_kept")
        piece, piece_max, rowmax = sem("piece_scored"), sem("piece_max"), sem("row_max_ready")
        mx_turned, mx_kept = sem("max_turned"), sem("max_kept")
        scored, expd, weighed = sem("chunk_scored"), sem("chunk_exp"), sem("chunk_weighed")
        acc_kept, z_ready, o_ready = sem("acc_kept"), sem("z_ready"), sem("o_ready")
        oT_ready, oT_kept, wo_done = sem("oT_ready"), sem("oT_kept"), sem("wo_done")
        qkv_done, q2_kept, v2_kept = sem("qkv_done"), sem("q2_kept"), sem("v2_kept")
        k2_kept = sem("k2_kept")
        lam_in, lam_exp = sem("lambda_in"), sem("lambda_exp")
        dve_part, pool_part, s_done = sem("score_part_vector"), sem("score_part_pool"), sem("scores_done")
        shifted_ready, sexp = sem("shifted_ready"), sem("scores_exp")
        dif_ready, pv_dve, pv_pool, pv_done = sem("diff_ready"), sem("pv_part_vector"), sem("pv_part_pool"), sem("pv_done")
        sq_done = sem("square_done")
        logit_done, lg_ready, lex_done = sem("logits_done"), sem("logits_ready"), sem("logits_exp")
        gu_done, th_done, h_done = sem("gate_up_done"), sem("tanh_done"), sem("hidden_done")
        y_done, y_added = sem("down_done"), sem("expert_added")

        block = ctx.enter_context(nc.Block())

        def stack(p):
            return kstack[p // 4][:, p % 4, :]

        @block.sync
        def _(sp):
            for i in range(KCH):
                sl = slice(i * BANK, (i + 1) * BANK)
                sp.dma_start(ctx_raw[:, :, sl], ctxT[:, :, sl]).then_inc(ld_ctx[i], 16)
            sp.dma_start(wv_s[:], wv).then_inc(ld["wv"], 16)
            sp.dma_start(wg_s[:], wg).then_inc(ld["wg"], 16)

            def save(tile, m, part):
                sp.dma_start(scratch[m * P:(m + 1) * P, part, :], tile[:, m, :].bitcast(F32)).then_inc(k_saved[m], 16)

            sp.wait_ge(k_hi_done, KCH)
            save(k_hi, 0, 0)
            sp.wait_ge(k_lo_done, KCH)
            save(k_lo, 0, 2)
            sp.wait_ge(k_saved[0], 48)
            for p in range(4):
                src = scratch[32 * p:32 * p + 32].rearrange("r b k -> (r b) k")
                sp.dma_start(stack(p)[0:ROWS].bitcast(F32), src).then_inc(kst_loaded[p], 16)
            sp.wait_ge(k_hi_done, 2 * KCH)
            save(k_hi, 1, 0)
            sp.wait_ge(k_lo_done, 2 * KCH)
            save(k_lo, 1, 2)
            sp.wait_ge(k_saved[1], 48)
            sp.wait_ge(vproj, KB)
            for p in range(4, PAIRS):
                src = scratch[32 * p:32 * p + 32].rearrange("r b k -> (r b) k")
                sp.dma_start(stack(p)[0:ROWS].bitcast(F32), src).then_inc(kst_loaded[p], 16)
            sp.dma_start(wo_s[:], wo).then_inc(ld["wo"], 16)
            sp.dma_start(wqkv_s[:], wqkv).then_inc(ld["wqkv"], 16)
            sp.dma_start(wo2_s[:], wo2).then_inc(ld["wo2"], 16)

            def load_expert(e):
                sp.dma_start(gu_w[e][:], wgu[e]).then_inc(ld_exp[e], 16)
                sp.dma_start(dn_w[e][:], wdn[e]).then_inc(ld_exp[e], 16)

            load_expert(0)
            load_expert(1)
            sp.wait_ge(scored, CHUNKS // 2)
            load_expert(2)
            load_expert(3)
            sp.wait_ge(scored, CHUNKS)
            load_expert(4)
            load_expert(5)
            sp.wait_ge(weighed, CHUNKS)
            load_expert(6)
            load_expert(7)
            sp.wait_ge(y_added, E)
            sp.dma_start(out, x2[:]).then_inc(out_saved, 16)
            sp.wait_ge(out_saved, 16)

        @block.scalar
        def _(act):
            for dst, src, s in ((wk_s, wk, "wk"), (xs, x, "x"), (cs, cst, "cst"), (nw, norm_w, "nw"),
                                (wq_s, wqs, "wq")):
                act.dma_start(dst[:], src).then_inc(ld[s], 16)
            for i in range(KCH):
                act.wait_ge(ld_ctx[i], 16)
                sl = slice(i * BANK, (i + 1) * BANK)
                nc.scalar.activation(ctx_hi[:, :, sl], ctx_raw[:, :, sl], ACT.Copy).then_inc(ctx_hi_done, 1)
            for i in range(2 * KCH):
                m, ch = divmod(i, KCH)
                act.wait_ge(kproj, i + 1)
                nc.scalar.activation(k_hi[:, m, ch * BANK:(ch + 1) * BANK], ps[:, i % 4, :],
                                     ACT.Copy).then_inc(k_hi_done, 1)
                if i % KCH == KCH - 1:
                    act.wait_ge(k_hi_done, i + 1)
                    act.dma_start(scratch[m * P:(m + 1) * P, 1, :], k_hi[:, m, :].bitcast(F32)).then_inc(k_saved[m], 16)
            act.wait_ge(gproj, 1)
            nc.scalar.activation(gate[:], ps[:, 5, 0:C], ACT.Tanh, scale=0.5).then_inc(g_kept, 1)
            act.wait_ge(lam_in, 2)
            nc.scalar.activation(lexp[:], lsum[:], ACT.Exp).then_inc(lam_exp, 1)
            for kb in range(0, KB, 2):
                act.wait_ge(vproj, kb + 1)
                nc.scalar.activation(vals[:, kb, :, 0:HD],
                                     ps[:, 4, 0:C].rearrange("p (h d) -> p h d", h=NH), ACT.Copy).then_inc(v_even, 1)

            def keep_max(p):
                act.wait_ge(mx_turned, p + 1)
                nc.scalar.activation(qstack[ONES_ROW:ONES_ROW + 1, p, :, :],
                                     ps[ONES_ROW:ONES_ROW + 1, 2, 0:2 * T].rearrange("o (j t) -> o j t", j=2),
                                     ACT.Copy).then_inc(mx_kept, 1)

            keep_max(0)
            for g in range(CHUNKS):
                act.wait_ge(scored, g + 1)
                if g >= PT:
                    act.wait_ge(weighed, g - PT + 1)
                nc.scalar.activation(probs[:, g % PT, :], ps[:, 4 + g % 2, :], ACT.Exp).then_inc(expd, 1)
                if g % 8 == 5 and g // 8 + 1 < PAIRS:
                    keep_max(g // 8 + 1)
            act.wait_ge(oT_ready, 1)
            nc.scalar.activation(oT[:], ps[:, 1, 0:C].rearrange("p (c t) -> p c t", c=KC), ACT.Copy).then_inc(oT_kept, 1)
            act.wait_ge(xT_ready, 2)
            nc.scalar.activation(x1T[:], ps[:, 3, 0:C].rearrange("p (c t) -> p c t", c=KC), ACT.Copy).then_inc(xT_kept, 1)
            act.wait_ge(qkv_done, 1)
            nc.scalar.activation(qd[:], ps[:, 4, 0:C].rearrange("p (d s) -> p d s", d=D2), ACT.Copy,
                                 scale=D2 ** -0.5).then_inc(q2_kept, 1)
            act.wait_ge(qkv_done, 2)
            nc.scalar.activation(vd[:], ps[:, 5, 0:C].rearrange("p (h d) -> p h d", h=NH), ACT.Copy).then_inc(v2_kept, 1)
            act.wait_ge(shifted_ready, 1)
            nc.scalar.activation(shifted[:], shifted[:], ACT.Exp).then_inc(sexp, 1)
            act.wait_ge(pv_done, 1)
            nc.scalar.activation(sq[:], ps[:, 0, 0:C].rearrange("p (h d) -> p h d", h=NH), ACT.Square).then_inc(sq_done, 1)
            act.wait_ge(oT_ready, 2)
            nc.scalar.activation(oT[:], ps[:, 1, 0:C].rearrange("p (c t) -> p c t", c=KC), ACT.Copy).then_inc(oT_kept, 1)
            act.wait_ge(xT_ready, 3)
            nc.scalar.activation(x2T[:], ps[:, 3, 0:C].rearrange("p (c t) -> p c t", c=KC), ACT.Copy).then_inc(xT_kept, 1)
            act.wait_ge(lg_ready, 1)
            nc.scalar.activation(lex[:], lex[:], ACT.Exp).then_inc(lex_done, 1)
            for e in range(E):
                act.wait_ge(gu_done, e + 1)
                if e >= 2:
                    act.wait_ge(h_done, e - 1)
                nc.scalar.activation(th[:, e % 2, :], ps[:, 4 + e % 2, :], ACT.Tanh, scale=0.5).then_inc(th_done, 1)

        @block.gpsimd
        def _(pool):
            chain = [0]

            def link(ins):
                chain[0] += 1
                ins.then_inc(pchain, 1)
                pool.wait_ge(pchain, chain[0])

            pool.dma_start(mask_u8[ONES_ROW:MASK_ROW + 1, :], mask2).then_inc(ld["mask"], 16)
            for dst, src in ((bo_s, bo), (lam_s, lams), (wr_s, wr)):
                pool.dma_start(dst[:], src).then_inc(ld["small"], 16)

            def root(col, src, eps):
                link(nc.gpsimd.tensor_scalar(rstd[:, col:col + 1], src, 1.0, eps, ALU.mult, ALU.add))
                nc.gpsimd.tensor_tensor(rstd[:, col:col + 1], rstd[:, col:col + 1], cs[:, C_PW:C_PW + 1],
                                        ALU.pow).then_inc(rstd_ready, 1)

            pool.wait_ge(ld["cst"], 16)
            pool.wait_ge(var_ready, 1)
            root(0, mv[:, 0, 1:2], LN_EPS)
            pool.wait_ge(var_ready, 2)
            pool.wait_ge(rstd_ready, 1)
            root(0, ms[:, 0:1], RMS_EPS)
            pool.wait_ge(rstd_ready, 2)
            pool.wait_ge(ld["mask"], 16)

            def const_rows(p):
                r = slice(ONES_ROW, KROWS)
                nc.gpsimd.tensor_scalar(stack(p)[r], mask_u8[r, :], cs[r, C_KS:C_KS + 1], cs[r, C_KB:C_KB + 1],
                                        ALU.mult, ALU.add).then_inc(kst_const, 1)
                pool.wait_ge(kst_const, p + 1)

            const_rows(0)
            pool.wait_ge(ld["wv"], 16)
            link(nc.gpsimd.tensor_copy(wv_hi[:], wv_s[:]))
            nc.gpsimd.tensor_tensor(wv_lo[:], wv_s[:], wv_hi[:].bitcast(F32), ALU.subtract).then_inc(wv_split, 1)
            pool.wait_ge(wv_split, 1)
            pool.wait_ge(q_kept, 4)
            rows = qstack[ONES_ROW:KROWS, :, :, :].bitcast(F32)
            link(nc.gpsimd.memset(rows, 1.0))
            nc.gpsimd.memset(qstack[ONES_ROW:ONES_ROW + 1, :, :, :].bitcast(F32), 0.0).then_inc(q_rows, 1)
            pool.wait_ge(q_rows, 1)
            pool.wait_ge(ctx_lo_done, KCH)
            pool.wait_ge(ctx_hi_done, KCH)
            nc.gpsimd.memset(vals[:, :, :, HD:HD + 1], 1.0).then_inc(v_pads, 1)
            nc.gpsimd.memset(vals[:, :, :, HD + 1:VW], 0.0).then_inc(v_pads, 1)
            pool.wait_ge(v_pads, 2)
            for p in range(1, 4):
                const_rows(p)
            pool.wait_ge(vproj, KB)
            for p in range(4, PAIRS):
                const_rows(p)

            pool.wait_ge(var_ready, 3)
            root(1, mv[:, 1, 1:2], LN_EPS)
            pool.wait_ge(q2_kept, 1)
            pool.wait_ge(k2_kept, 1)
            pool.wait_ge(weighed, CHUNKS)

            def product(buf, d):
                return nc.gpsimd.tensor_tensor(prod[buf][:].rearrange("p (a b) -> p a b", a=SUB),
                                               qd[:, d, :].unsqueeze(2).broadcast_to([P, SUB, SUB]),
                                               kd[:, d, :].unsqueeze(1).broadcast_to([P, SUB, SUB]), ALU.mult)

            product(5, 5).then_inc(pool_part, 1)
            link(product(6, 6))
            link(product(7, 7))
            nc.gpsimd.tensor_tensor(prod[6][:], prod[6][:], prod[7][:], ALU.add).then_inc(pool_part, 1)
            pool.wait_ge(dif_ready, 1)
            pool.wait_ge(s_done, 1)
            pool.wait_ge(v2_kept, 1)
            link(nc.gpsimd.tensor_tensor(
                prod[6][:, 0:512].rearrange("p (h a d) -> p h a d", h=2, a=NH),
                dif[:, :, 12:14].rearrange("p a h -> p h a").unsqueeze(3).broadcast_to([P, 2, NH, HD]),
                vd[:, 12:14, :].unsqueeze(2).broadcast_to([P, 2, NH, HD]), ALU.mult))
            link(nc.gpsimd.tensor_tensor(
                prod[7][:, 0:512].rearrange("p (h a d) -> p h a d", h=2, a=NH),
                dif[:, :, 14:16].rearrange("p a h -> p h a").unsqueeze(3).broadcast_to([P, 2, NH, HD]),
                vd[:, 14:16, :].unsqueeze(2).broadcast_to([P, 2, NH, HD]), ALU.mult))
            nc.gpsimd.tensor_tensor(prod[6][:, 0:512], prod[6][:, 0:512], prod[7][:, 0:512],
                                    ALU.add).then_inc(pv_pool, 1)
            pool.wait_ge(var_ready, 4)
            link(nc.gpsimd.tensor_scalar(rms[:], ssq[:], 1.0 / HD, LN_EPS, ALU.mult, ALU.add))
            nc.gpsimd.tensor_tensor(rms[:], rms[:], cs[:, C_PW:C_PW + 1].broadcast_to([P, NH]),
                                    ALU.pow).then_inc(rstd_ready, 1)
            pool.wait_ge(var_ready, 5)
            root(2, mv[:, 2, 1:2], LN_EPS)

        @block.tensor
        def _(pe):
            def split_product(dst, a_hi, a_lo, b_hi, b_lo):
                for kc in range(KC):
                    for n, (a, b) in enumerate(((a_hi, b_hi), (a_lo, b_hi), (a_hi, b_lo))):
                        last = nc.tensor.matmul(dst, a(kc), b(kc), start=(kc == 0 and n == 0),
                                                stop=(kc == KC - 1 and n == 2))
                return last

            def key_projection(i):
                m, ch = divmod(i, KCH)
                if m == 0:
                    pe.wait_ge(ctx_hi_done, ch + 1)
                    pe.wait_ge(ctx_lo_done, ch + 1)
                if i >= 4:
                    pe.wait_ge(k_hi_done, i - 3)
                    pe.wait_ge(k_lo_done, i - 3)
                rows, keys = slice(m * P, (m + 1) * P), slice(ch * BANK, (ch + 1) * BANK)
                split_product(ps[:, i % 4, :],
                              lambda kc: wk_hi[:, kc, rows], lambda kc: wk_lo[:, kc, rows],
                              lambda kc: ctx_hi[:, kc, keys], lambda kc: ctx_lo[:, kc, keys]).then_inc(kproj, 1)

            def value_projection(kb):
                if kb == 0:
                    pe.wait_ge(wv_split, 1)
                    pe.wait_ge(g_kept, 1)
                if kb >= 2:
                    pe.wait_ge(v_odd if kb % 2 else v_even, kb // 2)
                keys = slice(kb * P, (kb + 1) * P)
                split_product(ps[:, 4 + kb % 2, 0:C],
                              lambda kc: ctx_hi[:, kc, keys], lambda kc: ctx_lo[:, kc, keys],
                              lambda kc: wv_hi[:, kc, :], lambda kc: wv_lo[:, kc, :]).then_inc(vproj, 1)

            def turn(bank, src):
                for kc in range(KC):
                    last = nc.tensor.transpose(ps[:, bank, kc * T:(kc + 1) * T], src[:, kc * P:(kc + 1) * P], ident)
                return last

            def project(dst, lhs, w, cols):
                for kc in range(KC):
                    last = nc.tensor.matmul(dst, lhs[:, kc, :], w[:, kc, cols], start=(kc == 0), stop=(kc == KC - 1))
                return last

            def max_piece(a):
                h, half = divmod(a, 2)
                p, j = divmod(h, 2)
                if a % 4 == 0:
                    pe.wait_ge(kst_loaded[p], 16)
                    pe.wait_ge(kst_const, p + 1)
                if a == 0:
                    pe.wait_ge(q_rows, 1)
                    pe.wait_ge(k_hi_done, 2 * KCH)
                    pe.wait_ge(k_lo_done, 2 * KCH)
                if a >= 2:
                    pe.wait_ge(piece_max, a - 1)
                if a >= 5 and a % 4 == 1:
                    pe.wait_ge(mx_kept, a // 4)
                for n in range(2):
                    keys = slice(half * HALF + n * BANK, half * HALF + (n + 1) * BANK)
                    last = nc.tensor.matmul(ps[:, 2 * (a % 2) + n, :], qstack[0:KROWS, p, j, :], stack(p)[0:KROWS, keys],
                                            start=True, stop=True)
                last.then_inc(piece, 1)

            def turn_max(p):
                pe.wait_ge(rowmax, 2 * p + 2)
                for j in range(2):
                    last = nc.tensor.matmul(ps[ONES_ROW:ONES_ROW + 1, 2, j * T:(j + 1) * T],
                                            row_max[:, 2 * p + j:2 * p + j + 1], nident, start=True, stop=True)
                last.then_inc(mx_turned, 1)

            def score(g):
                p, c = divmod(g, KB // 2)
                if g < 2:
                    pe.wait_ge(v_even, KB // 2)
                    pe.wait_ge(v_odd, KB // 2)
                if g >= 2:
                    pe.wait_ge(expd, g - 1)
                if c == 0:
                    pe.wait_ge(mx_kept, p + 1)
                for n in range(2):
                    kb = 2 * c + n
                    last = nc.tensor.matmul(ps[:, 4 + g % 2, n * 2 * T:(n + 1) * 2 * T],
                                            stack(p)[0:KROWS, kb * P:(kb + 1) * P], qstack[0:KROWS, p, :, :],
                                            start=True, stop=True)
                last.then_inc(scored, 1)

            def weigh(g):
                p, c = divmod(g, KB // 2)
                pe.wait_ge(expd, g + 1)
                if g == 0:
                    pe.wait_ge(v_pads, 2)
                for n in range(2):
                    kb = 2 * c + n
                    for j in range(2):
                        row = 32 * (2 * j + n)
                        last = nc.tensor.matmul(ps[row:row + VW, 6 + p // 4, (p % 4) * T:(p % 4 + 1) * T],
                                                vals[:, kb, 2 * p + j, :], probs[:, g % PT, (2 * n + j) * T:(2 * n + j + 1) * T],
                                                start=(c == 0), stop=(c == KB // 2 - 1), skip_group_check=True)
                last.then_inc(weighed, 1)

            pe.wait_ge(wk_split, 2)
            for i in range(4):
                key_projection(i)
            pe.wait_ge(xn_ready, 1)
            pe.wait_ge(ld["cst"], 16)
            turn(7, h2).then_inc(xT_ready, 1)
            for i in range(4, 8):
                key_projection(i)
            pe.wait_ge(xT_kept, 1)
            pe.wait_ge(ld["wq"], 16)
            for p in range(PAIRS):
                for kc in range(KC):
                    last = nc.tensor.matmul(ps[0:KROWS, 6 + p // 4, (p % 4) * T:(p % 4 + 1) * T], wq_s[:, kc, p, :],
                                            xnT[:, kc, :], start=(kc == 0), stop=(kc == KC - 1))
            last.then_inc(qproj, 1)
            pe.wait_ge(ld["wg"], 16)
            project(ps[:, 5, 0:C], xnT, wg_s, slice(0, C)).then_inc(gproj, 1)
            for kb in range(KB):
                value_projection(kb)
                if kb >= 6 and kb % 2 == 0:
                    max_piece(kb // 2 - 3)
            turn_max(0)
            max_piece(5)
            for g in range(CHUNKS + 2):
                a = 6 + g // 2
                if g % 2 == 0 and a < NPIECE:
                    max_piece(a)
                if g < CHUNKS:
                    score(g)
                if g % 8 == 5 and g // 8 + 1 < PAIRS:
                    turn_max(g // 8 + 1)
                if g >= 2:
                    weigh(g - 2)
            pe.wait_ge(acc_kept, 2)
            for p in range(PAIRS):
                last = nc.tensor.matmul(ps[:, 0, p * 64:(p + 1) * 64], acc_s[:, p, :], cs[:, C_SEL:C_SEL + 64],
                                        start=True, stop=True)
            last.then_inc(z_ready, 1)
            pe.wait_ge(o_ready, 1)
            turn(1, o1[:].rearrange("p h d -> p (h d)")).then_inc(oT_ready, 1)
            pe.wait_ge(oT_kept, 1)
            pe.wait_ge(ld["wo"], 16)
            project(ps[:, 2, 0:C], oT, wo_s, slice(0, C)).then_inc(wo_done, 1)
            pe.wait_ge(xn_ready, 2)
            turn(3, x1n).then_inc(xT_ready, 1)
            pe.wait_ge(xT_kept, 2)
            pe.wait_ge(ld["wqkv"], 16)
            project(ps[:, 4, :], x1T, wqkv_s, slice(0, 2 * C)).then_inc(qkv_done, 1)
            project(ps[:, 5, 0:C], x1T, wqkv_s, slice(2 * C, 3 * C)).then_inc(qkv_done, 1)

            parts = [(dve_part, 1, 0), (pool_part, 1, 5), (dve_part, 2, 1), (pool_part, 2, 6), (dve_part, 3, 3)]
            for n, (who, count, buf) in enumerate(parts):
                pe.wait_ge(who, count)
                for half in range(2):
                    last = nc.tensor.matmul(ps[:, 6 + half, :], ident, prod[buf][:, half * BANK:(half + 1) * BANK],
                                            start=(n == 0), stop=(n == len(parts) - 1))
            last.then_inc(s_done, 1)
            pieces = [(pv_dve, 1, 0, 4), (pv_pool, 1, 6, 2), (pv_dve, 2, 2, 2)]
            total = sum(k for *_, k in pieces)
            n = 0
            for who, count, buf, k in pieces:
                pe.wait_ge(who, count)
                for i in range(k):
                    last = nc.tensor.matmul(ps[:, 0, 0:C], ident, prod[buf][:, i * C:(i + 1) * C],
                                            start=(n == 0), stop=(n == total - 1))
                    n += 1
            last.then_inc(pv_done, 1)
            pe.wait_ge(o_ready, 2)
            turn(1, o1[:].rearrange("p h d -> p (h d)")).then_inc(oT_ready, 1)
            pe.wait_ge(oT_kept, 2)
            pe.wait_ge(ld["wo2"], 16)
            project(ps[:, 2, 0:C], oT, wo2_s, slice(0, C)).then_inc(wo_done, 1)
            pe.wait_ge(xn_ready, 3)
            turn(3, x2n).then_inc(xT_ready, 1)
            pe.wait_ge(xT_kept, 3)
            pe.wait_ge(ld["small"], 48)
            project(ps[:, 2, 0:E], x2T, wr_s, slice(0, E)).then_inc(logit_done, 1)

            def gate_up(e):
                pe.wait_ge(ld_exp[e], 32)
                if e >= 2:
                    pe.wait_ge(h_done, e - 1)
                for half in range(2):
                    for ic in range(IC):
                        for kc in range(KC):
                            col = half * I + ic * P
                            last = nc.tensor.matmul(ps[:, 4 + 2 * half + e % 2, ic * T:(ic + 1) * T],
                                                    gu_w[e][:, kc, col:col + P], x2T[:, kc, :],
                                                    start=(kc == 0), stop=(kc == KC - 1))
                last.then_inc(gu_done, 1)

            def down(e):
                pe.wait_ge(h_done, e + 1)
                if e >= 2:
                    pe.wait_ge(y_added, e - 1)
                for ic in range(IC):
                    last = nc.tensor.matmul(ps[:, e % 2, 0:C], hT[:, e % 2, ic * T:(ic + 1) * T], dn_w[e][:, ic, :],
                                            start=(ic == 0), stop=(ic == IC - 1))
                last.then_inc(y_done, 1)

            gate_up(0)
            for e in range(E):
                if e + 1 < E:
                    gate_up(e + 1)
                down(e)

        @block.vector
        def _(dve):
            chain = [0]

            def link(ins):
                chain[0] += 1
                ins.then_inc(vchain, 1)
                dve.wait_ge(vchain, chain[0])

            dve.wait_ge(ld["wk"], 16)
            nc.vector.tensor_copy(wk_hi[:], wk_s[:]).then_inc(wk_split, 1)
            dve.wait_ge(wk_split, 1)
            nc.vector.tensor_tensor(wk_lo[:], wk_s[:], wk_hi[:].bitcast(F32), ALU.subtract).then_inc(wk_split, 1)

            def context_rest(i):
                dve.wait_ge(ctx_hi_done, i + 1)
                sl = slice(i * BANK, (i + 1) * BANK)
                nc.vector.tensor_tensor(ctx_lo[:, :, sl], ctx_raw[:, :, sl], ctx_hi[:, :, sl].bitcast(F32),
                                        ALU.subtract).then_inc(ctx_lo_done, 1)

            def key_rest(i):
                m, ch = divmod(i, KCH)
                dve.wait_ge(k_hi_done, i + 1)
                sl = slice(ch * BANK, (ch + 1) * BANK)
                nc.vector.tensor_tensor(k_lo[:, m, sl], ps[:, i % 4, :], k_hi[:, m, sl].bitcast(F32),
                                        ALU.subtract).then_inc(k_lo_done, 1)

            def moments(n, src):
                link(nc.vector.bn_stats(stat[:, n, :], src))
                nc.vector.bn_aggr(mv[:, n, :], stat[:, n, :]).then_inc(var_ready, 1)

            context_rest(0)
            dve.wait_ge(ld["x"], 16)
            moments(0, xs[:])
            context_rest(1)
            dve.wait_ge(rstd_ready, 1)
            dve.wait_ge(var_ready, 1)
            link(nc.vector.tensor_scalar(hn[:], xs[:], mv[:, 0, 0:1], rstd[:, 0:1], ALU.subtract, ALU.mult))
            nc.vector.tensor_tensor_reduce(out=junk[:], in0=hn[:], in1=hn[:], scale=1.0 / C, scalar=0.0,
                                           op0=ALU.mult, op1=ALU.add, accum_out=ms[:, 0:1]).then_inc(var_ready, 1)
            context_rest(2)
            key_rest(0)
            dve.wait_ge(rstd_ready, 2)
            nc.vector.tensor_scalar(h2[:], hn[:], rstd[:, 0:1], None, ALU.mult).then_inc(xn_ready, 1)
            context_rest(3)
            for i in range(1, 4):
                key_rest(i)
            dve.wait_ge(xT_ready, 1)
            dve.wait_ge(ld["nw"], 16)
            for kc in range(KC):
                last = nc.vector.tensor_scalar(xnT[:, kc, :], ps[:, 7, kc * T:(kc + 1) * T], nw[:, kc:kc + 1], None,
                                               ALU.mult)
                link(last)
            nc.vector.engine_nop().then_inc(xT_kept, 1)
            for i in range(4, 8):
                key_rest(i)
            dve.wait_ge(qproj, 1)
            qp = ps[0:ROWS, 6:8, :].rearrange("r b (p t) -> r (b p) t", t=T)
            for j in range(2):
                link(nc.vector.tensor_scalar(qneg[0:ROWS, j], qp, cs[0:ROWS, C_S0 + j:C_S0 + j + 1], None, ALU.mult))
                nc.vector.scalar_tensor_tensor(qstack[0:ROWS, :, j, :], qp, cs[0:ROWS, C_M0 + j:C_M0 + j + 1],
                                               qneg[0:ROWS, j].bitcast(F32), ALU.mult, ALU.add).then_inc(q_kept, 2)
            dve.wait_ge(g_kept, 1)
            link(nc.vector.tensor_scalar(gate[:], gate[:], 0.5, 0.5, ALU.mult, ALU.add))
            dve.wait_ge(ld["small"], 48)
            for n in range(2):
                nc.vector.tensor_tensor_reduce(out=junk[:, n * D2:(n + 1) * D2], in0=lam_s[:, 2 * n, :],
                                               in1=lam_s[:, 2 * n + 1, :], scale=1.0, scalar=0.0, op0=ALU.mult,
                                               op1=ALU.add, accum_out=lsum[:, n:n + 1]).then_inc(lam_in, 1)
            dve.wait_ge(lam_exp, 1)
            link(nc.vector.tensor_scalar(nlam[:], lexp[:, 1:2], lexp[:, 0:1], LAM_INIT, ALU.subtract, ALU.subtract))

            def reduce_piece(a):
                dve.wait_ge(piece, a + 1)
                nc.vector.tensor_reduce(part_max[:, a:a + 1], ps[:, 2 * (a % 2):2 * (a % 2) + 2, :], AX.XY,
                                        ALU.max).then_inc(piece_max, 1)
                if a % 2 == 1:
                    dve.wait_ge(piece_max, a + 1)
                    nc.vector.tensor_scalar(row_max[:, a // 2:a // 2 + 1], part_max[:, a - 1:a], part_max[:, a:a + 1],
                                            FLOOR, ALU.max, ALU.max).then_inc(rowmax, 1)

            done = 0
            for kb in range(1, KB, 2):
                dve.wait_ge(vproj, kb + 1)
                nc.vector.tensor_copy(vals[:, kb, :, 0:HD],
                                      ps[:, 5, 0:C].rearrange("p (h d) -> p h d", h=NH)).then_inc(v_odd, 1)
                if kb >= 7:
                    reduce_piece(done)
                    done += 1
            for a in range(done, NPIECE):
                reduce_piece(a)
                if a == 24:
                    dve.wait_ge(weighed, CHUNKS // 2)
                    nc.vector.tensor_copy(acc_s[:, 0:4, :], ps[:, 6, :].rearrange("p (c t) -> p c t", c=4)).then_inc(acc_kept, 1)
            dve.wait_ge(weighed, CHUNKS)
            nc.vector.tensor_copy(acc_s[:, 4:8, :], ps[:, 7, :].rearrange("p (c t) -> p c t", c=4)).then_inc(acc_kept, 1)
            dve.wait_ge(z_ready, 1)
            z = ps[:, 0, :].rearrange("p (h w) -> p h w", h=NH)
            link(nc.vector.tensor_scalar(den[:], z[:, :, HD], 1e-30, None, ALU.max))
            link(nc.vector.reciprocal(rden[:], den[:]))
            nc.vector.tensor_tensor(o1[:], z[:, :, 0:HD], rden[:].unsqueeze(2).broadcast_to([P, NH, HD]),
                                    ALU.mult).then_inc(o_ready, 1)
            dve.wait_ge(wo_done, 1)
            link(nc.vector.tensor_tensor(junk[:], ps[:, 2, 0:C], gate[:], ALU.mult))
            link(nc.vector.tensor_tensor(x1[:], junk[:], xs[:], ALU.add))
            moments(1, x1[:])
            nc.vector.tensor_tensor(x1b[:], x1[:], bo_s[:], ALU.add).then_inc(vchain, 1)
            chain[0] += 1
            dve.wait_ge(rstd_ready, 3)
            dve.wait_ge(var_ready, 3)
            nc.vector.tensor_scalar(x1n[:], x1[:], mv[:, 1, 0:1], rstd[:, 1:2], ALU.subtract, ALU.mult).then_inc(xn_ready, 1)
            dve.wait_ge(qkv_done, 2)
            dve.wait_ge(q2_kept, 1)
            nc.vector.tensor_copy(kd[:], ps[:, 4, C:2 * C].rearrange("p (d s) -> p d s", d=D2)).then_inc(k2_kept, 1)
            dve.wait_ge(k2_kept, 1)

            def product(buf, d):
                return nc.vector.tensor_tensor(prod[buf][:].rearrange("p (a b) -> p a b", a=SUB),
                                               qd[:, d, :].unsqueeze(2).broadcast_to([P, SUB, SUB]),
                                               kd[:, d, :].unsqueeze(1).broadcast_to([P, SUB, SUB]), ALU.mult)

            product(0, 0).then_inc(dve_part, 1)
            for b in (1, 3):
                link(product(b, b))
                link(product(b + 1, b + 1))
                nc.vector.tensor_tensor(prod[b][:], prod[b][:], prod[b + 1][:], ALU.add).then_inc(dve_part, 1)
            dve.wait_ge(s_done, 1)
            sc = ps[:, 6:8, :].rearrange("p b (a k) -> p (b a) k", k=SUB)
            link(nc.vector.tensor_reduce(smax[:], sc, AX.X, ALU.max))
            link(nc.vector.tensor_scalar(smax[:], smax[:], FMAX, -FMAX, ALU.min, ALU.max))
            for b in range(2):
                nc.vector.scalar_tensor_tensor(shifted[:, b * NH:(b + 1) * NH, :], sc[:, b * NH:(b + 1) * NH, :], FMAX,
                                               smax[:, b * NH:(b + 1) * NH].unsqueeze(2).broadcast_to([P, NH, SUB]),
                                               ALU.min, ALU.subtract).then_inc(vchain, 1)
                chain[0] += 1
            dve.wait_ge(vchain, chain[0])
            nc.vector.engine_nop().then_inc(shifted_ready, 1)
            dve.wait_ge(sexp, 1)
            link(nc.vector.tensor_reduce(ssum[:], shifted[:], AX.X, ALU.add))
            link(nc.vector.reciprocal(srec[:], ssum[:]))
            link(nc.vector.tensor_scalar(srec[:, NH:SUB], srec[:, NH:SUB], nlam[:, 0:1], None, ALU.mult))
            link(nc.vector.tensor_tensor(dif[:], shifted[:, 0:NH, 0:NH],
                                         srec[:, 0:NH].unsqueeze(2).broadcast_to([P, NH, NH]), ALU.mult))
            link(nc.vector.tensor_tensor(dif1[:], shifted[:, NH:SUB, NH:SUB],
                                         srec[:, NH:SUB].unsqueeze(2).broadcast_to([P, NH, NH]), ALU.mult))
            nc.vector.tensor_tensor(dif[:], dif[:], dif1[:], ALU.add).then_inc(dif_ready, 1)
            dve.wait_ge(dif_ready, 1)
            dve.wait_ge(v2_kept, 1)

            def weighted(buf, h0, n):
                return nc.vector.tensor_tensor(
                    prod[buf][:, 0:n * C].rearrange("p (h a d) -> p h a d", h=n, a=NH),
                    dif[:, :, h0:h0 + n].rearrange("p a h -> p h a").unsqueeze(3).broadcast_to([P, n, NH, HD]),
                    vd[:, h0:h0 + n, :].unsqueeze(2).broadcast_to([P, n, NH, HD]), ALU.mult)

            for buf, h0, n in ((0, 0, 4), (2, 8, 2)):
                link(weighted(buf, h0, n))
                link(weighted(buf + 1, h0 + n, n))
                nc.vector.tensor_tensor(prod[buf][:, 0:n * C], prod[buf][:, 0:n * C], prod[buf + 1][:, 0:n * C],
                                        ALU.add).then_inc(pv_dve, 1)
            dve.wait_ge(sq_done, 1)
            nc.vector.tensor_reduce(ssq[:], sq[:], AX.X, ALU.add).then_inc(var_ready, 1)
            dve.wait_ge(rstd_ready, 4)
            link(nc.vector.tensor_scalar(rms[:], rms[:], 1.0 - LAM_INIT, None, ALU.mult))
            nc.vector.tensor_tensor(o1[:], ps[:, 0, 0:C].rearrange("p (h d) -> p h d", h=NH),
                                    rms[:].unsqueeze(2).broadcast_to([P, NH, HD]), ALU.mult).then_inc(o_ready, 1)
            dve.wait_ge(wo_done, 2)
            link(nc.vector.tensor_tensor(x2[:], ps[:, 2, 0:C], x1b[:], ALU.add))
            moments(2, x2[:])
            dve.wait_ge(rstd_ready, 5)
            dve.wait_ge(var_ready, 5)
            nc.vector.tensor_scalar(x2n[:], x2[:], mv[:, 2, 0:1], rstd[:, 2:3], ALU.subtract, ALU.mult).then_inc(xn_ready, 1)
            dve.wait_ge(logit_done, 1)
            link(nc.vector.tensor_copy(lg[:], ps[:, 2, 0:E]))
            link(nc.vector.tensor_reduce(lmax[:], lg[:], AX.X, ALU.max))
            nc.vector.tensor_scalar(lex[:], lg[:], lmax[:, 0:1], None, ALU.subtract).then_inc(lg_ready, 1)
            mine, other = lg[:].unsqueeze(2).broadcast_to([P, E, E]), lg[:].unsqueeze(1).broadcast_to([P, E, E])
            link(nc.vector.tensor_tensor(rk[:], other, mine, ALU.is_gt))
            link(nc.vector.tensor_tensor(rk2[:], other, mine, ALU.is_equal))
            link(nc.vector.tensor_tensor(rk2[:], rk2[:], cs[:, C_TRI:C_ALL].rearrange("p (i j) -> p i j", i=E), ALU.mult))
            link(nc.vector.tensor_tensor(rk[:], rk[:], rk2[:], ALU.add))
            link(nc.vector.tensor_reduce(rank[:], rk[:], AX.X, ALU.add))
            dve.wait_ge(lex_done, 1)
            link(nc.vector.scalar_tensor_tensor(wsel[:], rank[:], 2.0, lex[:], ALU.is_lt, ALU.mult))
            link(nc.vector.tensor_reduce(wsum[:, 0:1], wsel[:], AX.X, ALU.add))
            link(nc.vector.reciprocal(wsum[:, 1:2], wsum[:, 0:1]))
            link(nc.vector.tensor_scalar(wsel[:], wsel[:], wsum[:, 1:2], 0.5, ALU.mult, ALU.mult))

            def hidden(e):
                dve.wait_ge(th_done, e + 1)
                if e >= 2:
                    dve.wait_ge(y_done, e - 1)
                link(nc.vector.scalar_tensor_tensor(hT[:, e % 2, :], th[:, e % 2, :], 1.0, ps[:, 4 + e % 2, :],
                                                    ALU.add, ALU.mult))
                nc.vector.tensor_tensor(hT[:, e % 2, :], hT[:, e % 2, :], ps[:, 6 + e % 2, :], ALU.mult).then_inc(h_done, 1)

            def add_expert(e):
                dve.wait_ge(y_done, e + 1)
                if e >= 1:
                    dve.wait_ge(y_added, e)
                nc.vector.scalar_tensor_tensor(x2[:], ps[:, e % 2, 0:C], wsel[:, e:e + 1], x2[:], ALU.mult,
                                               ALU.add).then_inc(y_added, 1)

            hidden(0)
            for e in range(E):
                if e + 1 < E:
                    hidden(e + 1)
                add_expert(e)


def _turned(w, rows=slice(None)):
    w = np.asarray(w)[rows]
    return np.ascontiguousarray(w.T.reshape(-1, P, w.shape[0]).transpose(1, 0, 2))


def kernel(**inputs):
    import concourse.bacc as _bacc
    from concourse.bass_utils import run_bass_kernel_spmd as _run

    a = {k: np.asarray(v) for k, v in inputs.items()}
    dup = np.repeat(np.arange(NH * HD), 3).reshape(PAIRS, ROWS)
    wq = _turned(a["L0_xattn_wq"])
    wqs = np.zeros((P, KC, PAIRS, KROWS), np.float32)
    wqs[..., :ROWS] = wq[:, :, dup]
    sub = np.arange(C).reshape(NH, D2, 2).transpose(1, 2, 0).reshape(-1)
    wqkv = np.concatenate([_turned(a["L0_attn_Wq"], sub), _turned(a["L0_attn_Wk"], sub), _turned(a["L0_attn_Wv"])], axis=2)
    lams = np.stack([a["L0_attn_lq1"], a["L0_attn_lk1"], a["L0_attn_lq2"], a["L0_attn_lk2"]])
    gu = a["L0_ffn_gate_up_proj"]
    dn = a["L0_ffn_down_proj"]
    arrays = {
        "x": a["x"][0],
        "ctxT": _turned(a["ctx_2048"][0]),
        "mask2": np.broadcast_to(a["mask_BxS2_bk0"], (2, S)),
        "cst": constants(),
        "norm_w": a["L0_xattn_norm_w"].reshape(KC, P).T,
        "wk": _turned(a["L0_xattn_wk"]),
        "wv": _turned(a["L0_xattn_wv"]),
        "wqs": wqs,
        "wg": _turned(a["L0_xattn_wg"]),
        "wo": _turned(a["L0_xattn_wo"]),
        "wqkv": wqkv,
        "wo2": _turned(a["L0_attn_Wo"]),
        "bo": np.broadcast_to(a["L0_attn_bo"], (P, C)),
        "lams": np.broadcast_to(lams, (P, 4, D2)),
        "wr": _turned(a["L0_ffn_gate_weight"]),
        "wgu": np.stack([_turned(gu[e]) for e in range(E)]),
        "wdn": np.stack([_turned(dn[e]) for e in range(E)]),
    }
    nc = _bacc.Bacc("TRN2", target_bir_lowering=False, num_devices=1)
    feed, args = {}, []
    for name, v in arrays.items():
        v = np.ascontiguousarray(v)
        feed[f"in_{name}"] = v
        args.append(nc.dram_tensor(f"in_{name}", v.shape, mybir.dt.from_np(v.dtype), kind="ExternalInput").ap())
    out = nc.dram_tensor("out_0", (T, C), F32, kind="ExternalOutput").ap()
    perceiver_layer(nc, *args, out)
    r = _run(nc, [feed], core_ids=[0])
    return r.results[0]["out_0"].reshape(1, T, C)
```

```python
from contextlib import ExitStack

import numpy as np

import concourse.bass as bass
from concourse import mybir

F32 = mybir.dt.float32
F32R = mybir.dt.float32r
U8 = mybir.dt.uint8
ALU = mybir.AluOpType
ACT = mybir.ActivationFunctionType
AX = mybir.AxisListType

P = 128
T = 128
C = 256
KC = C // P
S = 2048
NH, HD = 16, 16
PAIRS = NH // 2
ROWS = 2 * HD * 3
ONES_ROW, MASK_ROW = ROWS, ROWS + 1
KROWS = ROWS + 2
BANK = 512
KCH = S // BANK
KB = S // P
HALF = 2 * BANK
NPIECE = NH * S // HALF
CHUNKS = PAIRS * KB // 2
PT = 4
VW = 32
D2 = HD // 2
SUB = 2 * NH
E, I = 8, 512
IC = I // P
MASKED = -float(2.0 ** 100)
FLOOR = -float(2.0 ** 96)
FMAX = 3.4028234663852886e38
LAM_INIT = 0.8 - 0.6 * float(np.exp(-0.3 * 12))
LN_EPS, RMS_EPS = 1e-5, 1e-6

C_M0, C_M1, C_S0, C_S1, C_KS, C_KB, C_PW = range(7)
C_ID = 8
C_NEG = C_ID + P
C_SEL = C_NEG + P
C_TRI = C_SEL + 64
C_ALL = C_TRI + E * E


def constants():
    c = np.zeros((P, C_ALL), np.float32)
    r = np.arange(ROWS)
    scale = HD ** -0.5
    for j in range(2):
        own = (r // (ROWS // 2)) == j
        c[:ROWS, C_M0 + j] = own * scale
        c[:ROWS, C_S0 + j] = (own & (r % 3 == 1)) * -scale
    c[ONES_ROW, C_KS], c[ONES_ROW, C_KB] = 0.0, 1.0
    c[MASK_ROW, C_KS], c[MASK_ROW, C_KB] = -MASKED, MASKED
    c[:, C_PW] = -0.5
    c[:, C_ID:C_ID + P] = np.eye(P)
    c[:, C_NEG:C_NEG + P] = -np.eye(P)
    q = np.arange(P)
    c[q, C_SEL + 32 * (q // 64) + q % 32] = 1.0
    c[:, C_TRI:C_TRI + E * E] = np.tril(np.ones((E, E)), -1).reshape(-1)
    return c


def perceiver_layer(nc, x, ctxT, mask2, cst, norm_w, wk, wv, wqs, wg, wo, wqkv, wo2, bo, lams, wr, wgu, wdn, out):
    with ExitStack() as ctx:
        def sb(name, shape, dt=F32):
            return ctx.enter_context(nc.sbuf_tensor(name, shape, dt))

        def sem(name):
            return ctx.enter_context(nc.semaphore(name))

        base = (nc.sbuf_base + 63) // 64 * 64
        KIB = 1024
        arena = sb("arena", [P, 151 * KIB // 4 + 16])

        def at(name, shape, kib, dt=F32):
            return nc.alloc_sbuf_tensor_at(name, shape, dt, offset=base + kib * KIB)

        kstack = [at("kstack_a", [P, 4, S], 0, F32R), at("kstack_b", [P, 4, S], 32, F32R)]
        ctx_hi = at("ctx_hi", [P, KC, S], 32, F32R)
        ctx_lo = at("ctx_lo", [P, KC, S], 48, F32R)
        vals = at("vals", [P, KB, NH, VW], 64)
        ctx_raw = at("ctx_raw", [P, KC, S], 64)
        k_hi = at("k_hi", [P, 2, S], 96, F32R)
        k_lo = at("k_lo", [P, 2, S], 112, F32R)
        probs = at("probs", [P, PT, BANK], 128)
        qneg = at("qneg", [KROWS, 2, PAIRS, T], 128, F32R)
        qstack = at("qstack", [P, PAIRS, 2, T], 136, F32R)
        w_at = [96, 108, 0, 12, 32, 44, 64, 76]
        gu_w = [at(f"gate_up{e}", [P, KC, 2 * I], w_at[e]) for e in range(E)]
        dn_w = [at(f"down{e}", [P, IC, C], w_at[e] + 8) for e in range(E)]
        prod = [at(f"prod{i}", [P, 1024], kib) for i, kib in enumerate([24, 28, 56, 60, 88, 92, 120, 124])]
        shifted = at("shifted", [P, SUB, SUB], 128)
        wq_s = at("wq_s", [P, KC, PAIRS, KROWS], 144)
        wqkv_hi, wqkv_lo = at("wqkv_hi", [P, KC, 3 * C], 120, F32R), at("wqkv_lo", [P, KC, 3 * C], 144, F32R)
        th, hT = at("th", [P, 2, I], 24), at("hT", [P, 2, I], 28)

        cs = sb("cs", [P, C_ALL])
        ident, nident = cs[:, C_ID:C_ID + P], cs[:, C_NEG:C_NEG + P]
        nw = sb("nw", [P, KC])
        xs = sb("xs", [P, C])
        mask_u8 = sb("mask_u8", [P, S], U8)
        wk_s, wk_hi, wk_lo = sb("wk_s", [P, KC, C]), sb("wk_hi", [P, KC, C], F32R), sb("wk_lo", [P, KC, C], F32R)
        wv_s, wv_hi, wv_lo = sb("wv_s", [P, KC, C]), sb("wv_hi", [P, KC, C], F32R), sb("wv_lo", [P, KC, C], F32R)
        wg_s, wo_s, wo2_s = sb("wg_s", [P, KC, C]), sb("wo_s", [P, KC, C]), sb("wo2_s", [P, KC, C])
        wqkv_s = sb("wqkv_s", [P, KC, 3 * C])
        bo_s, lam_s, wr_s = sb("bo_s", [P, C]), sb("lam_s", [P, 4, D2]), sb("wr_s", [P, KC, E])
        warm = sb("warm", [P, 1])
        stat, mv, rstd, ms = sb("stat", [P, 3, 6]), sb("mv", [P, 3, 2]), sb("rstd", [P, 3]), sb("ms", [P, 2])
        junk, hn, h2 = sb("junk", [P, C]), sb("hn", [P, C]), sb("h2", [P, C])
        xnT = sb("xnT", [P, KC, T])
        gate = sb("gate", [P, C])
        part_max, row_max = sb("part_max", [P, NPIECE]), sb("row_max", [P, NH])
        acc_s = sb("acc_s", [P, PAIRS, T])
        den, rden = sb("den", [P, NH]), sb("rden", [P, NH])
        wo_hi, wo_lo, wo2_hi, wo2_lo = wk_hi, wk_lo, wv_hi, wv_lo
        o1 = sb("o1", [P, NH, HD])
        oT_hi, oT_lo = sb("oT_hi", [P, KC, T], F32R), sb("oT_lo", [P, KC, T], F32R)
        x1, x1b = sb("x1", [P, C]), sb("x1b", [P, C])
        x1T_hi, x1T_lo = sb("x1T_hi", [P, KC, T], F32R), sb("x1T_lo", [P, KC, T], F32R)
        qd, kd, vd = sb("qd", [P, D2, SUB]), sb("kd", [P, D2, SUB]), sb("vd", [P, NH, HD])
        smax, ssum, srec = sb("smax", [P, SUB]), sb("ssum", [P, SUB]), sb("srec", [P, SUB])
        dif, dif1 = sb("dif", [P, NH, NH]), sb("dif1", [P, NH, NH])
        lsum, lexp, nlam = sb("lsum", [P, 2]), sb("lexp", [P, 2]), sb("nlam", [P, 1])
        sq, ssq, rms = sb("sq", [P, NH, HD]), sb("ssq", [P, NH]), sb("rms", [P, NH])
        x2, x2T = sb("x2", [P, C]), sb("x2T", [P, KC, T])
        x1n = x2n = h2
        lg, rk, rk2 = sb("lg", [P, E]), sb("rk", [P, E, E]), sb("rk2", [P, E, E])
        rank, lmax, lex, wsel, wsum = sb("rank", [P, E]), sb("lmax", [P, 1]), sb("lex", [P, E]), sb("wsel", [P, E]), sb("wsum", [P, 2])

        ps = ctx.enter_context(nc.psum_tensor("ps", [P, 8, BANK], F32))
        scratch = nc.dram_tensor("k_parts", [2 * P, 3, S], F32)

        ld = {n: sem("loaded_" + n) for n in
              ("x", "cst", "wk", "wv", "wq", "wg", "nw", "mask", "wo", "wqkv", "wo2", "small")}
        ld_ctx = [sem(f"loaded_ctx{i}") for i in range(KCH)]
        ld_exp = [sem(f"loaded_expert{e}") for e in range(E)]
        k_saved = [sem(f"k_saved{m}") for m in range(2)]
        kst_loaded = [sem(f"kstack_loaded{p}") for p in range(PAIRS)]
        out_saved = sem("out_saved")
        vchain, achain, pchain = sem("vector_chain"), sem("scalar_chain"), sem("pool_chain")
        warm_in = sem("warm_in")
        wk_split, wv_split = sem("wk_split"), sem("wv_split")
        ctx_hi_done, ctx_lo_done = sem("ctx_hi_done"), sem("ctx_lo_done")
        kproj, k_hi_done, k_lo_done = sem("k_projected"), sem("k_hi_done"), sem("k_lo_done")
        vproj, v_kept = sem("v_projected"), sem("v_kept")
        v_pads = sem("v_pads")
        kst_const = sem("kstack_constant_rows")
        var_ready, rstd_ready = sem("variance_ready"), sem("rstd_ready")
        xn_ready, xT_ready, xT_kept = sem("xn_ready"), sem("xT_ready"), sem("xT_kept")
        qproj, q_kept, q_rows = sem("q_projected"), sem("q_kept"), sem("q_constant_rows")
        gproj, g_kept = sem("gate_projected"), sem("gate_kept")
        piece, piece_max, rowmax = sem("piece_scored"), sem("piece_max"), sem("row_max_ready")
        mx_turned, mx_kept = sem("max_turned"), sem("max_kept")
        scored, expd, weighed = sem("chunk_scored"), sem("chunk_exp"), sem("chunk_weighed")
        acc_kept, z_ready, o_ready = sem("acc_kept"), sem("z_ready"), sem("o_ready")
        oT_ready, oT_kept, wo_done = sem("oT_ready"), sem("oT_kept"), sem("wo_done")
        qkv_done, q2_kept, v2_kept = sem("qkv_done"), sem("q2_kept"), sem("v2_kept")
        k2_kept = sem("k2_kept")
        w_split = sem("late_weights_split")
        oT_rest, x1T_rest = sem("oT_rest_kept"), sem("x1T_rest_kept")
        lam_in, lam_exp = sem("lambda_in"), sem("lambda_exp")
        dve_part, pool_part, s_done = sem("score_part_vector"), sem("score_part_pool"), sem("scores_done")
        shifted_ready, sexp = sem("shifted_ready"), sem("scores_exp")
        dif_ready, pv_dve, pv_pool, pv_done = sem("diff_ready"), sem("pv_part_vector"), sem("pv_part_pool"), sem("pv_done")
        sq_done = sem("square_done")
        logit_done, lg_ready, lex_done = sem("logits_done"), sem("logits_ready"), sem("logits_exp")
        gu_done, th_done, h_done = sem("gate_up_done"), sem("tanh_done"), sem("hidden_done")
        y_done, y_added = sem("down_done"), sem("expert_added")

        block = ctx.enter_context(nc.Block())

        def stack(p):
            return kstack[p // 4][:, p % 4, :]

        @block.sync
        def _(sp):
            def load(dst, src, name):
                sp.dma_start(dst, src).then_inc(ld[name], 16)

            def load_context(i):
                sl = slice(i * BANK, (i + 1) * BANK)
                sp.dma_start(ctx_raw[:, :, sl], ctxT[:, :, sl]).then_inc(ld_ctx[i], 16)

            load(wk_s[:], wk, "wk")
            load_context(0)
            load_context(1)
            load_context(2)
            load(mask_u8[ONES_ROW:MASK_ROW + 1, :], mask2, "mask")
            load(xs[:], x, "x")
            load(cs[:], cst, "cst")
            load_context(3)
            load(nw[:], norm_w, "nw")
            load(wv_s[:], wv, "wv")
            load(wq_s[:], wqs, "wq")
            load(wg_s[:], wg, "wg")

            def save(m, half):
                sl = slice(half * HALF, (half + 1) * HALF)
                sp.wait_ge(k_hi_done, KCH * m + 2 * half + 2)
                sp.dma_start(scratch[m * P:(m + 1) * P, 0, sl], k_hi[:, m, sl].bitcast(F32)).then_inc(k_saved[m], 16)
                sp.wait_ge(k_lo_done, KCH * m + 2 * half + 2)
                sp.dma_start(scratch[m * P:(m + 1) * P, 2, sl], k_lo[:, m, sl].bitcast(F32)).then_inc(k_saved[m], 16)

            save(0, 0)
            save(0, 1)
            for dst, src in ((bo_s, bo), (lam_s, lams), (wr_s, wr)):
                load(dst[:], src, "small")
            sp.wait_ge(k_saved[0], 96)
            for p in range(4):
                src = scratch[32 * p:32 * p + 32].rearrange("r b k -> (r b) k")
                sp.dma_start(stack(p)[0:ROWS].bitcast(F32), src).then_inc(kst_loaded[p], 16)
            save(1, 0)
            save(1, 1)
            sp.wait_ge(k_saved[1], 96)
            sp.wait_ge(vproj, KB)
            for p in range(4, PAIRS):
                src = scratch[32 * p:32 * p + 32].rearrange("r b k -> (r b) k")
                sp.dma_start(stack(p)[0:ROWS].bitcast(F32), src).then_inc(kst_loaded[p], 16)
            sp.dma_start(wo_s[:], wo).then_inc(ld["wo"], 16)
            sp.dma_start(wqkv_s[:], wqkv).then_inc(ld["wqkv"], 16)
            sp.dma_start(wo2_s[:], wo2).then_inc(ld["wo2"], 16)

            def load_expert(e):
                sp.dma_start(gu_w[e][:], wgu[e]).then_inc(ld_exp[e], 16)
                sp.dma_start(dn_w[e][:], wdn[e]).then_inc(ld_exp[e], 16)

            load_expert(0)
            load_expert(1)
            sp.wait_ge(scored, CHUNKS // 2)
            load_expert(2)
            load_expert(3)
            sp.wait_ge(scored, CHUNKS)
            load_expert(4)
            load_expert(5)
            sp.wait_ge(weighed, CHUNKS)
            load_expert(6)
            load_expert(7)
            sp.wait_ge(y_added, E)
            sp.dma_start(out, x2[:]).then_inc(out_saved, 16)
            sp.wait_ge(out_saved, 16)

        @block.scalar
        def _(act):
            act.wait_ge(warm_in, 1)
            nc.scalar.activation(warm[:], warm[:], ACT.Copy).then_inc(achain, 1)

            def context_hi(i):
                sl = slice(i * BANK, (i + 1) * BANK)
                act.wait_ge(ld_ctx[i], 16)
                for kc in range(KC):
                    nc.scalar.activation(ctx_hi[:, kc, sl], ctx_raw[:, kc, sl], ACT.Copy).then_inc(ctx_hi_done, 1)

            def key_hi(i):
                m, ch = divmod(i, KCH)
                act.wait_ge(kproj, i + 1)
                nc.scalar.activation(k_hi[:, m, ch * BANK:(ch + 1) * BANK], ps[:, i % 4, :],
                                     ACT.Copy).then_inc(k_hi_done, 1)
                if i % 2 == 1:
                    sl = slice((ch - 1) * BANK, (ch + 1) * BANK)
                    act.wait_ge(k_hi_done, i + 1)
                    act.dma_start(scratch[m * P:(m + 1) * P, 1, sl], k_hi[:, m, sl].bitcast(F32)).then_inc(k_saved[m], 16)

            context_hi(0)
            context_hi(1)
            for i in range(2 * KCH):
                if i + 2 < KCH:
                    context_hi(i + 2)
                key_hi(i)
            act.wait_ge(gproj, 1)
            nc.scalar.activation(gate[:], ps[:, 5, 0:C], ACT.Tanh, scale=0.5).then_inc(g_kept, 1)
            act.wait_ge(ctx_lo_done, KC * KCH)
            act.wait_ge(ctx_hi_done, KC * KCH)
            for kb in range(KB):
                act.wait_ge(vproj, kb + 1)
                nc.scalar.activation(vals[:, kb, :, 0:HD],
                                     ps[:, 4 + kb % 2, 0:C].rearrange("p (h d) -> p h d", h=NH),
                                     ACT.Copy).then_inc(v_kept, 1)

            def keep_max(p):
                act.wait_ge(mx_turned, p + 1)
                nc.scalar.activation(qstack[ONES_ROW:ONES_ROW + 1, p, :, :],
                                     ps[ONES_ROW:ONES_ROW + 1, 2, 0:2 * T].rearrange("o (j t) -> o j t", j=2),
                                     ACT.Copy).then_inc(mx_kept, 1)

            keep_max(0)
            for g in range(CHUNKS):
                act.wait_ge(scored, g + 1)
                if g >= PT:
                    act.wait_ge(weighed, g - PT + 1)
                nc.scalar.activation(probs[:, g % PT, :], ps[:, 4 + g % 2, :], ACT.Exp).then_inc(expd, 1)
                if g % 8 == 5 and g // 8 + 1 < PAIRS:
                    keep_max(g // 8 + 1)
            act.wait_ge(lam_in, 2)
            nc.scalar.activation(lexp[:], lsum[:], ACT.Exp).then_inc(lam_exp, 1)
            act.wait_ge(oT_ready, 1)
            nc.scalar.activation(oT_hi[:], ps[:, 1, 0:C].rearrange("p (c t) -> p c t", c=KC), ACT.Copy).then_inc(oT_kept, 1)
            act.wait_ge(xT_ready, 2)
            nc.scalar.activation(x1T_hi[:], ps[:, 3, 0:C].rearrange("p (c t) -> p c t", c=KC), ACT.Copy).then_inc(xT_kept, 1)
            act.wait_ge(qkv_done, 1)
            nc.scalar.activation(qd[:], ps[:, 4, 0:C].rearrange("p (d s) -> p d s", d=D2), ACT.Copy,
                                 scale=D2 ** -0.5).then_inc(q2_kept, 1)
            act.wait_ge(qkv_done, 3)
            nc.scalar.activation(vd[:], ps[:, 1, 0:C].rearrange("p (h d) -> p h d", h=NH), ACT.Copy).then_inc(v2_kept, 1)
            for half in range(2):
                act.wait_ge(shifted_ready, half + 1)
                rows = slice(half * NH, (half + 1) * NH)
                nc.scalar.activation(shifted[:, rows, :], shifted[:, rows, :], ACT.Exp).then_inc(sexp, 1)
            act.wait_ge(pv_done, 1)
            nc.scalar.activation(sq[:], ps[:, 0, 0:C].rearrange("p (h d) -> p h d", h=NH), ACT.Square).then_inc(sq_done, 1)
            act.wait_ge(oT_ready, 2)
            nc.scalar.activation(oT_hi[:], ps[:, 1, 0:C].rearrange("p (c t) -> p c t", c=KC), ACT.Copy).then_inc(oT_kept, 1)
            act.wait_ge(xT_ready, 3)
            nc.scalar.activation(x2T[:], ps[:, 3, 0:C].rearrange("p (c t) -> p c t", c=KC), ACT.Copy).then_inc(xT_kept, 1)
            act.wait_ge(lg_ready, 1)
            nc.scalar.activation(lex[:], lex[:], ACT.Exp).then_inc(lex_done, 1)
            for e in range(E):
                act.wait_ge(gu_done, e + 1)
                if e >= 2:
                    act.wait_ge(h_done, e - 1)
                nc.scalar.activation(th[:, e % 2, :], ps[:, 4 + e % 2, :], ACT.Tanh, scale=0.5).then_inc(th_done, 1)

        @block.gpsimd
        def _(pool):
            chain = [0]

            def link(ins):
                chain[0] += 1
                ins.then_inc(pchain, 1)
                pool.wait_ge(pchain, chain[0])

            nc.gpsimd.memset(warm[:], 0.0).then_inc(warm_in, 1)
            pool.wait_ge(warm_in, 1)
            rows = qstack[ONES_ROW:KROWS, :, :, :].bitcast(F32)
            link(nc.gpsimd.memset(rows, 1.0))
            nc.gpsimd.memset(qstack[ONES_ROW:ONES_ROW + 1, :, :, :].bitcast(F32), 0.0).then_inc(q_rows, 1)
            pool.wait_ge(q_rows, 1)

            def root(col, src, eps):
                link(nc.gpsimd.tensor_scalar(rstd[:, col:col + 1], src, 1.0, eps, ALU.mult, ALU.add))
                nc.gpsimd.tensor_tensor(rstd[:, col:col + 1], rstd[:, col:col + 1], cs[:, C_PW:C_PW + 1],
                                        ALU.pow).then_inc(rstd_ready, 1)

            def const_rows(p):
                r = slice(ONES_ROW, KROWS)
                nc.gpsimd.tensor_scalar(stack(p)[r], mask_u8[r, :], cs[r, C_KS:C_KS + 1], cs[r, C_KB:C_KB + 1],
                                        ALU.mult, ALU.add).then_inc(kst_const, 1)
                pool.wait_ge(kst_const, p + 1)

            pool.wait_ge(ld["mask"], 16)
            pool.wait_ge(ld["cst"], 16)
            const_rows(0)
            pool.wait_ge(var_ready, 1)
            root(0, mv[:, 0, 1:2], LN_EPS)
            pool.wait_ge(var_ready, 2)
            pool.wait_ge(rstd_ready, 1)
            root(0, ms[:, 0:1], RMS_EPS)
            pool.wait_ge(rstd_ready, 2)
            pool.wait_ge(ld["wv"], 16)
            link(nc.gpsimd.tensor_copy(wv_hi[:], wv_s[:]))
            nc.gpsimd.tensor_tensor(wv_lo[:], wv_s[:], wv_hi[:].bitcast(F32), ALU.subtract).then_inc(wv_split, 1)
            pool.wait_ge(wv_split, 1)
            pool.wait_ge(ctx_lo_done, KC * KCH)
            pool.wait_ge(ctx_hi_done, KC * KCH)
            nc.gpsimd.memset(vals[:, :, :, HD:HD + 1], 1.0).then_inc(v_pads, 1)
            nc.gpsimd.memset(vals[:, :, :, HD + 1:VW], 0.0).then_inc(v_pads, 1)
            pool.wait_ge(v_pads, 2)
            for p in range(1, 4):
                const_rows(p)
            pool.wait_ge(vproj, KB)
            for p in range(4, PAIRS):
                const_rows(p)

            for name, w, hi, lo in (("wo", wo_s, wo_hi[:], wo_lo[:]), ("wqkv", wqkv_s, wqkv_hi[:], wqkv_lo[:]),
                                    ("wo2", wo2_s, wo2_hi[:], wo2_lo[:])):
                pool.wait_ge(ld[name], 16)
                link(nc.gpsimd.tensor_copy(hi, w[:]))
                nc.gpsimd.tensor_tensor(lo, w[:], hi.bitcast(F32), ALU.subtract).then_inc(w_split, 1)

            pool.wait_ge(w_split, 3)
            pool.wait_ge(var_ready, 3)
            root(1, mv[:, 1, 1:2], LN_EPS)
            pool.wait_ge(q2_kept, 1)
            pool.wait_ge(k2_kept, 1)
            pool.wait_ge(weighed, CHUNKS)

            def product(half, d):
                rows = slice(half * NH, (half + 1) * NH)
                return nc.gpsimd.tensor_tensor(prod[d][:, half * BANK:(half + 1) * BANK].rearrange("p (a b) -> p a b", a=NH),
                                               qd[:, d, rows].unsqueeze(2).broadcast_to([P, NH, SUB]),
                                               kd[:, d, :].unsqueeze(1).broadcast_to([P, NH, SUB]), ALU.mult)

            pool.wait_ge(qkv_done, 3)
            for half in range(2):
                cols = slice(half * BANK, (half + 1) * BANK)
                product(half, 5).then_inc(pool_part, 1)
                link(product(half, 6))
                link(product(half, 7))
                nc.gpsimd.tensor_tensor(prod[6][:, cols], prod[6][:, cols], prod[7][:, cols], ALU.add).then_inc(pool_part, 1)
                pool.wait_ge(pool_part, 2 * half + 2)
            pool.wait_ge(dif_ready, 1)
            pool.wait_ge(s_done, 2)
            pool.wait_ge(v2_kept, 1)
            link(nc.gpsimd.tensor_tensor(
                prod[6][:, 0:512].rearrange("p (h a d) -> p h a d", h=2, a=NH),
                dif[:, :, 12:14].rearrange("p a h -> p h a").unsqueeze(3).broadcast_to([P, 2, NH, HD]),
                vd[:, 12:14, :].unsqueeze(2).broadcast_to([P, 2, NH, HD]), ALU.mult))
            link(nc.gpsimd.tensor_tensor(
                prod[7][:, 0:512].rearrange("p (h a d) -> p h a d", h=2, a=NH),
                dif[:, :, 14:16].rearrange("p a h -> p h a").unsqueeze(3).broadcast_to([P, 2, NH, HD]),
                vd[:, 14:16, :].unsqueeze(2).broadcast_to([P, 2, NH, HD]), ALU.mult))
            nc.gpsimd.tensor_tensor(prod[6][:, 0:512], prod[6][:, 0:512], prod[7][:, 0:512],
                                    ALU.add).then_inc(pv_pool, 1)
            pool.wait_ge(var_ready, 4)
            link(nc.gpsimd.tensor_scalar(rms[:], ssq[:], 1.0 / HD, LN_EPS, ALU.mult, ALU.add))
            nc.gpsimd.tensor_tensor(rms[:], rms[:], cs[:, C_PW:C_PW + 1].broadcast_to([P, NH]),
                                    ALU.pow).then_inc(rstd_ready, 1)
            pool.wait_ge(var_ready, 5)
            root(2, mv[:, 2, 1:2], LN_EPS)

        @block.tensor
        def _(pe):
            def split_product(dst, a_hi, a_lo, b_hi, b_lo, ready=lambda n, kc: None):
                for n, (a, b) in enumerate(((a_hi, b_hi), (a_lo, b_hi), (a_hi, b_lo))):
                    for kc in range(KC):
                        ready(n, kc)
                        last = nc.tensor.matmul(dst, a(kc), b(kc), start=(kc == 0 and n == 0),
                                                stop=(kc == KC - 1 and n == 2))
                return last

            def key_projection(i):
                m, ch = divmod(i, KCH)

                def ready(n, kc):
                    if m == 0 and n == 0:
                        pe.wait_ge(ctx_hi_done, KC * ch + kc + 1)
                    if m == 0 and n == 2:
                        pe.wait_ge(ctx_lo_done, KC * ch + kc + 1)
                    if i == 0 and n == 1 and kc == 0:
                        pe.wait_ge(wk_split, 2)

                if i >= 4:
                    pe.wait_ge(k_hi_done, i - 3)
                    pe.wait_ge(k_lo_done, i - 3)
                rows, keys = slice(m * P, (m + 1) * P), slice(ch * BANK, (ch + 1) * BANK)
                split_product(ps[:, i % 4, :],
                              lambda kc: wk_hi[:, kc, rows], lambda kc: wk_lo[:, kc, rows],
                              lambda kc: ctx_hi[:, kc, keys], lambda kc: ctx_lo[:, kc, keys],
                              ready).then_inc(kproj, 1)

            def value_projection(kb):
                if kb == 0:
                    pe.wait_ge(wv_split, 1)
                if kb == 1:
                    pe.wait_ge(g_kept, 1)
                if kb >= 2:
                    pe.wait_ge(v_kept, kb - 1)
                keys = slice(kb * P, (kb + 1) * P)
                split_product(ps[:, 4 + kb % 2, 0:C],
                              lambda kc: ctx_hi[:, kc, keys], lambda kc: ctx_lo[:, kc, keys],
                              lambda kc: wv_hi[:, kc, :], lambda kc: wv_lo[:, kc, :]).then_inc(vproj, 1)

            def turn(bank, src):
                for kc in range(KC):
                    last = nc.tensor.transpose(ps[:, bank, kc * T:(kc + 1) * T], src[:, kc * P:(kc + 1) * P], ident)
                return last

            def project(dst, lhs, w, cols):
                for kc in range(KC):
                    last = nc.tensor.matmul(dst, lhs[:, kc, :], w[:, kc, cols], start=(kc == 0), stop=(kc == KC - 1))
                return last

            def project_split(dst, hi, lo, w_hi, w_lo, cols):
                return split_product(dst, lambda kc: hi[:, kc, :], lambda kc: lo[:, kc, :],
                                     lambda kc: w_hi[:, kc, cols], lambda kc: w_lo[:, kc, cols])

            def keep_clock(n, bank=0):
                for _ in range(n):
                    nc.tensor.matmul(ps[:, bank, 0:P], ident, ident, start=True, stop=True)

            def max_piece(a):
                h, half = divmod(a, 2)
                p, j = divmod(h, 2)
                if a % 4 == 0:
                    pe.wait_ge(kst_loaded[p], 16)
                    pe.wait_ge(kst_const, p + 1)
                if a == 0:
                    pe.wait_ge(q_rows, 1)
                    pe.wait_ge(q_kept, 4)
                    pe.wait_ge(k_hi_done, 2 * KCH)
                    pe.wait_ge(k_lo_done, 2 * KCH)
                if a >= 2:
                    pe.wait_ge(piece_max, a - 1)
                if a >= 5 and a % 4 == 1:
                    pe.wait_ge(mx_kept, a // 4)
                for n in range(2):
                    keys = slice(half * HALF + n * BANK, half * HALF + (n + 1) * BANK)
                    last = nc.tensor.matmul(ps[:, 2 * (a % 2) + n, :], qstack[0:KROWS, p, j, :], stack(p)[0:KROWS, keys],
                                            start=True, stop=True)
                last.then_inc(piece, 1)

            def turn_max(p):
                pe.wait_ge(rowmax, 2 * p + 2)
                for j in range(2):
                    last = nc.tensor.matmul(ps[ONES_ROW:ONES_ROW + 1, 2, j * T:(j + 1) * T],
                                            row_max[:, 2 * p + j:2 * p + j + 1], nident, start=True, stop=True)
                last.then_inc(mx_turned, 1)

            def score(g):
                p, c = divmod(g, KB // 2)
                if g < 2:
                    pe.wait_ge(v_kept, KB)
                if g >= 2:
                    pe.wait_ge(expd, g - 1)
                if c == 0:
                    pe.wait_ge(mx_kept, p + 1)
                for n in range(2):
                    kb = 2 * c + n
                    last = nc.tensor.matmul(ps[:, 4 + g % 2, n * 2 * T:(n + 1) * 2 * T],
                                            stack(p)[0:KROWS, kb * P:(kb + 1) * P], qstack[0:KROWS, p, :, :],
                                            start=True, stop=True)
                last.then_inc(scored, 1)

            def weigh(g):
                p, c = divmod(g, KB // 2)
                pe.wait_ge(expd, g + 1)
                if g == 0:
                    pe.wait_ge(v_pads, 2)
                for n in range(2):
                    kb = 2 * c + n
                    for j in range(2):
                        row = 32 * (2 * j + n)
                        last = nc.tensor.matmul(ps[row:row + VW, 6 + p // 4, (p % 4) * T:(p % 4 + 1) * T],
                                                vals[:, kb, 2 * p + j, :], probs[:, g % PT, (2 * n + j) * T:(2 * n + j + 1) * T],
                                                start=(c == 0), stop=(c == KB // 2 - 1), skip_group_check=True)
                last.then_inc(weighed, 1)

            pe.wait_ge(wk_split, 1)
            for i in range(6):
                key_projection(i)
            pe.wait_ge(xn_ready, 1)
            pe.wait_ge(ld["cst"], 16)
            turn(7, h2).then_inc(xT_ready, 1)
            for i in range(6, 8):
                key_projection(i)
            pe.wait_ge(xT_kept, 1)
            pe.wait_ge(ld["wq"], 16)
            for p in range(PAIRS):
                for kc in range(KC):
                    last = nc.tensor.matmul(ps[0:KROWS, 6 + p // 4, (p % 4) * T:(p % 4 + 1) * T], wq_s[:, kc, p, :],
                                            xnT[:, kc, :], start=(kc == 0), stop=(kc == KC - 1))
            last.then_inc(qproj, 1)
            pe.wait_ge(ld["wg"], 16)
            project(ps[:, 5, 0:C], xnT, wg_s, slice(0, C)).then_inc(gproj, 1)
            for kb in range(KB):
                value_projection(kb)
                if kb >= 6 and kb % 2 == 0:
                    max_piece(kb // 2 - 3)
            turn_max(0)
            max_piece(5)
            for g in range(0, CHUNKS + 2, 2):
                a = 6 + g // 2
                late = g % 8 == 6
                if a < NPIECE and not late:
                    max_piece(a)
                if g < CHUNKS:
                    score(g)
                    score(g + 1)
                if g >= 2:
                    weigh(g - 2)
                    weigh(g - 1)
                if g % 8 == 4 and g // 8 + 1 < PAIRS:
                    turn_max(g // 8 + 1)
                if a < NPIECE and late:
                    max_piece(a)
            keep_clock(4)
            pe.wait_ge(acc_kept, 2)
            for p in range(PAIRS):
                last = nc.tensor.matmul(ps[:, 0, p * 64:(p + 1) * 64], acc_s[:, p, :], cs[:, C_SEL:C_SEL + 64],
                                        start=True, stop=True)
            last.then_inc(z_ready, 1)
            pe.wait_ge(o_ready, 1)
            turn(1, o1[:].rearrange("p h d -> p (h d)")).then_inc(oT_ready, 1)
            pe.wait_ge(w_split, 1)
            pe.wait_ge(oT_kept, 1)
            pe.wait_ge(oT_rest, 1)
            project_split(ps[:, 2, 0:C], oT_hi, oT_lo, wo_hi, wo_lo, slice(0, C)).then_inc(wo_done, 1)
            keep_clock(12)
            pe.wait_ge(xn_ready, 2)
            turn(3, x1n).then_inc(xT_ready, 1)
            pe.wait_ge(w_split, 2)
            pe.wait_ge(xT_kept, 2)
            pe.wait_ge(x1T_rest, 1)
            for n, bank in enumerate((4, 5, 1)):
                project_split(ps[:, bank, 0:C], x1T_hi, x1T_lo, wqkv_hi, wqkv_lo,
                              slice(n * C, (n + 1) * C)).then_inc(qkv_done, 1)
            keep_clock(4)
            for half in range(2):
                parts = [(dve_part, 1, 0), (pool_part, 1, 5), (dve_part, 2, 1), (pool_part, 2, 6), (dve_part, 3, 3)]
                for n, (who, count, buf) in enumerate(parts):
                    pe.wait_ge(who, count + half * (3 if who is dve_part else 2))
                    last = nc.tensor.matmul(ps[:, 6 + half, :], ident, prod[buf][:, half * BANK:(half + 1) * BANK],
                                            start=(n == 0), stop=(n == len(parts) - 1))
                last.then_inc(s_done, 1)
            keep_clock(32)
            pieces = [(pv_dve, 1, 0, 4), (pv_pool, 1, 6, 2), (pv_dve, 2, 2, 2)]
            total = sum(k for *_, k in pieces)
            n = 0
            for who, count, buf, k in pieces:
                pe.wait_ge(who, count)
                for i in range(k):
                    last = nc.tensor.matmul(ps[:, 0, 0:C], ident, prod[buf][:, i * C:(i + 1) * C],
                                            start=(n == 0), stop=(n == total - 1))
                    n += 1
            last.then_inc(pv_done, 1)
            keep_clock(20, 3)
            pe.wait_ge(o_ready, 2)
            turn(1, o1[:].rearrange("p h d -> p (h d)")).then_inc(oT_ready, 1)
            pe.wait_ge(w_split, 3)
            pe.wait_ge(oT_kept, 2)
            pe.wait_ge(oT_rest, 2)
            project_split(ps[:, 2, 0:C], oT_hi, oT_lo, wo2_hi, wo2_lo, slice(0, C)).then_inc(wo_done, 1)
            keep_clock(8)
            pe.wait_ge(xn_ready, 3)
            turn(3, x2n).then_inc(xT_ready, 1)
            pe.wait_ge(xT_kept, 3)
            pe.wait_ge(ld["small"], 48)
            project(ps[:, 2, 0:E], x2T, wr_s, slice(0, E)).then_inc(logit_done, 1)

            def gate_up(e):
                pe.wait_ge(ld_exp[e], 32)
                if e >= 2:
                    pe.wait_ge(h_done, e - 1)
                for half in range(2):
                    for ic in range(IC):
                        for kc in range(KC):
                            col = half * I + ic * P
                            last = nc.tensor.matmul(ps[:, 4 + 2 * half + e % 2, ic * T:(ic + 1) * T],
                                                    gu_w[e][:, kc, col:col + P], x2T[:, kc, :],
                                                    start=(kc == 0), stop=(kc == KC - 1))
                last.then_inc(gu_done, 1)

            def down(e):
                pe.wait_ge(h_done, e + 1)
                if e >= 2:
                    pe.wait_ge(y_added, e - 1)
                for ic in range(IC):
                    last = nc.tensor.matmul(ps[:, e % 2, 0:C], hT[:, e % 2, ic * T:(ic + 1) * T], dn_w[e][:, ic, :],
                                            start=(ic == 0), stop=(ic == IC - 1))
                last.then_inc(y_done, 1)

            gate_up(0)
            for e in range(E):
                if e + 1 < E:
                    gate_up(e + 1)
                down(e)

        @block.vector
        def _(dve):
            chain = [0]

            def link(ins):
                chain[0] += 1
                ins.then_inc(vchain, 1)
                dve.wait_ge(vchain, chain[0])

            dve.wait_ge(ld["wk"], 16)
            nc.vector.tensor_copy(wk_hi[:], wk_s[:]).then_inc(wk_split, 1)
            dve.wait_ge(wk_split, 1)
            nc.vector.tensor_tensor(wk_lo[:], wk_s[:], wk_hi[:].bitcast(F32), ALU.subtract).then_inc(wk_split, 1)

            def context_rest(i):
                sl = slice(i * BANK, (i + 1) * BANK)
                for kc in range(KC):
                    dve.wait_ge(ctx_hi_done, KC * i + kc + 1)
                    nc.vector.tensor_tensor(ctx_lo[:, kc, sl], ctx_raw[:, kc, sl], ctx_hi[:, kc, sl].bitcast(F32),
                                            ALU.subtract).then_inc(ctx_lo_done, 1)

            def key_rest(i):
                m, ch = divmod(i, KCH)
                dve.wait_ge(k_hi_done, i + 1)
                sl = slice(ch * BANK, (ch + 1) * BANK)
                nc.vector.tensor_tensor(k_lo[:, m, sl], ps[:, i % 4, :], k_hi[:, m, sl].bitcast(F32),
                                        ALU.subtract).then_inc(k_lo_done, 1)

            def moments(n, src):
                link(nc.vector.bn_stats(stat[:, n, :], src))
                nc.vector.bn_aggr(mv[:, n, :], stat[:, n, :]).then_inc(var_ready, 1)

            context_rest(0)
            context_rest(1)
            context_rest(2)
            key_rest(0)
            dve.wait_ge(ld["x"], 16)
            moments(0, xs[:])
            context_rest(3)
            dve.wait_ge(rstd_ready, 1)
            dve.wait_ge(var_ready, 1)
            link(nc.vector.tensor_scalar(hn[:], xs[:], mv[:, 0, 0:1], rstd[:, 0:1], ALU.subtract, ALU.mult))
            nc.vector.tensor_tensor_reduce(out=junk[:], in0=hn[:], in1=hn[:], scale=1.0 / C, scalar=0.0,
                                           op0=ALU.mult, op1=ALU.add, accum_out=ms[:, 0:1]).then_inc(var_ready, 1)
            key_rest(1)
            dve.wait_ge(rstd_ready, 2)
            nc.vector.tensor_scalar(h2[:], hn[:], rstd[:, 0:1], None, ALU.mult).then_inc(xn_ready, 1)
            for i in range(2, 6):
                key_rest(i)
            dve.wait_ge(xT_ready, 1)
            dve.wait_ge(ld["nw"], 16)
            for kc in range(KC):
                last = nc.vector.tensor_scalar(xnT[:, kc, :], ps[:, 7, kc * T:(kc + 1) * T], nw[:, kc:kc + 1], None,
                                               ALU.mult)
                link(last)
            nc.vector.engine_nop().then_inc(xT_kept, 1)
            for i in range(6, 8):
                key_rest(i)
            dve.wait_ge(qproj, 1)
            qp = ps[0:ROWS, 6:8, :].rearrange("r b (p t) -> r (b p) t", t=T)
            for j in range(2):
                link(nc.vector.tensor_scalar(qneg[0:ROWS, j], qp, cs[0:ROWS, C_S0 + j:C_S0 + j + 1], None, ALU.mult))
                nc.vector.scalar_tensor_tensor(qstack[0:ROWS, :, j, :], qp, cs[0:ROWS, C_M0 + j:C_M0 + j + 1],
                                               qneg[0:ROWS, j].bitcast(F32), ALU.mult, ALU.add).then_inc(q_kept, 2)
            def reduce_piece(a):
                dve.wait_ge(piece, a + 1)
                nc.vector.tensor_reduce(part_max[:, a:a + 1], ps[:, 2 * (a % 2):2 * (a % 2) + 2, :], AX.XY,
                                        ALU.max).then_inc(piece_max, 1)
                if a % 2 == 1:
                    dve.wait_ge(piece_max, a + 1)
                    nc.vector.tensor_scalar(row_max[:, a // 2:a // 2 + 1], part_max[:, a - 1:a], part_max[:, a:a + 1],
                                            FLOOR, ALU.max, ALU.max).then_inc(rowmax, 1)

            for a in range(NPIECE):
                reduce_piece(a)
                if a == 24:
                    dve.wait_ge(weighed, CHUNKS // 2)
                    nc.vector.tensor_copy(acc_s[:, 0:4, :], ps[:, 6, :].rearrange("p (c t) -> p c t", c=4)).then_inc(acc_kept, 1)
            dve.wait_ge(g_kept, 1)
            link(nc.vector.tensor_scalar(gate[:], gate[:], 0.5, 0.5, ALU.mult, ALU.add))
            dve.wait_ge(ld["small"], 48)
            for n in range(2):
                nc.vector.tensor_tensor_reduce(out=junk[:, n * D2:(n + 1) * D2], in0=lam_s[:, 2 * n, :],
                                               in1=lam_s[:, 2 * n + 1, :], scale=1.0, scalar=0.0, op0=ALU.mult,
                                               op1=ALU.add, accum_out=lsum[:, n:n + 1]).then_inc(lam_in, 1)
            dve.wait_ge(weighed, CHUNKS)
            nc.vector.tensor_copy(acc_s[:, 4:8, :], ps[:, 7, :].rearrange("p (c t) -> p c t", c=4)).then_inc(acc_kept, 1)
            dve.wait_ge(lam_exp, 1)
            link(nc.vector.tensor_scalar(nlam[:], lexp[:, 1:2], lexp[:, 0:1], LAM_INIT, ALU.subtract, ALU.subtract))
            dve.wait_ge(z_ready, 1)
            z = ps[:, 0, :].rearrange("p (h w) -> p h w", h=NH)
            link(nc.vector.tensor_scalar(den[:], z[:, :, HD], 1e-30, None, ALU.max))
            link(nc.vector.reciprocal(rden[:], den[:]))
            nc.vector.tensor_tensor(o1[:], z[:, :, 0:HD], rden[:].unsqueeze(2).broadcast_to([P, NH, HD]),
                                    ALU.mult).then_inc(o_ready, 1)

            def rest(lo, hi, bank, kept, count, done):
                dve.wait_ge(kept, count)
                nc.vector.tensor_tensor(lo[:], ps[:, bank, 0:C].rearrange("p (c t) -> p c t", c=KC),
                                        hi[:].bitcast(F32), ALU.subtract).then_inc(done, 1)

            rest(oT_lo, oT_hi, 1, oT_kept, 1, oT_rest)
            dve.wait_ge(wo_done, 1)
            link(nc.vector.tensor_tensor(junk[:], ps[:, 2, 0:C], gate[:], ALU.mult))
            link(nc.vector.tensor_tensor(x1[:], junk[:], xs[:], ALU.add))
            moments(1, x1[:])
            nc.vector.tensor_tensor(x1b[:], x1[:], bo_s[:], ALU.add).then_inc(vchain, 1)
            chain[0] += 1
            dve.wait_ge(rstd_ready, 3)
            dve.wait_ge(var_ready, 3)
            nc.vector.tensor_scalar(x1n[:], x1[:], mv[:, 1, 0:1], rstd[:, 1:2], ALU.subtract, ALU.mult).then_inc(xn_ready, 1)
            rest(x1T_lo, x1T_hi, 3, xT_kept, 2, x1T_rest)
            dve.wait_ge(qkv_done, 2)
            nc.vector.tensor_copy(kd[:], ps[:, 5, 0:C].rearrange("p (d s) -> p d s", d=D2)).then_inc(k2_kept, 1)
            dve.wait_ge(k2_kept, 1)
            dve.wait_ge(q2_kept, 1)

            def product(half, d):
                rows = slice(half * NH, (half + 1) * NH)
                return nc.vector.tensor_tensor(prod[d][:, half * BANK:(half + 1) * BANK].rearrange("p (a b) -> p a b", a=NH),
                                               qd[:, d, rows].unsqueeze(2).broadcast_to([P, NH, SUB]),
                                               kd[:, d, :].unsqueeze(1).broadcast_to([P, NH, SUB]), ALU.mult)

            def scores_products(half):
                cols = slice(half * BANK, (half + 1) * BANK)
                product(half, 0).then_inc(dve_part, 1)
                for b in (1, 3):
                    product(half, b).then_inc(vchain, 1)
                    product(half, b + 1).then_inc(vchain, 1)
                    chain[0] += 2
                    dve.wait_ge(vchain, chain[0])
                    nc.vector.tensor_tensor(prod[b][:, cols], prod[b][:, cols], prod[b + 1][:, cols],
                                            ALU.add).then_inc(dve_part, 1)

            def softmax_shift(half):
                rows = slice(half * NH, (half + 1) * NH)
                sc = ps[:, 6 + half, :].rearrange("p (a k) -> p a k", k=SUB)
                dve.wait_ge(s_done, half + 1)
                link(nc.vector.tensor_reduce(smax[:, rows], sc, AX.X, ALU.max))
                link(nc.vector.tensor_scalar(smax[:, rows], smax[:, rows], FMAX, -FMAX, ALU.min, ALU.max))
                nc.vector.scalar_tensor_tensor(shifted[:, rows, :], sc, FMAX,
                                               smax[:, rows].unsqueeze(2).broadcast_to([P, NH, SUB]),
                                               ALU.min, ALU.subtract).then_inc(shifted_ready, 1)

            def softmax_sum(half):
                rows = slice(half * NH, (half + 1) * NH)
                dve.wait_ge(sexp, half + 1)
                link(nc.vector.tensor_reduce(ssum[:, rows], shifted[:, rows, :], AX.X, ALU.add))
                link(nc.vector.reciprocal(srec[:, rows], ssum[:, rows]))

            scores_products(0)
            scores_products(1)
            softmax_shift(0)
            softmax_shift(1)
            softmax_sum(0)
            nc.vector.tensor_tensor(dif[:], shifted[:, 0:NH, 0:NH],
                                    srec[:, 0:NH].unsqueeze(2).broadcast_to([P, NH, NH]), ALU.mult).then_inc(vchain, 1)
            chain[0] += 1
            softmax_sum(1)
            link(nc.vector.tensor_scalar(srec[:, NH:SUB], srec[:, NH:SUB], nlam[:, 0:1], None, ALU.mult))
            link(nc.vector.tensor_tensor(dif1[:], shifted[:, NH:SUB, NH:SUB],
                                         srec[:, NH:SUB].unsqueeze(2).broadcast_to([P, NH, NH]), ALU.mult))
            nc.vector.tensor_tensor(dif[:], dif[:], dif1[:], ALU.add).then_inc(dif_ready, 1)
            dve.wait_ge(dif_ready, 1)
            dve.wait_ge(v2_kept, 1)

            def weighted(buf, h0, n):
                return nc.vector.tensor_tensor(
                    prod[buf][:, 0:n * C].rearrange("p (h a d) -> p h a d", h=n, a=NH),
                    dif[:, :, h0:h0 + n].rearrange("p a h -> p h a").unsqueeze(3).broadcast_to([P, n, NH, HD]),
                    vd[:, h0:h0 + n, :].unsqueeze(2).broadcast_to([P, n, NH, HD]), ALU.mult)

            for buf, h0, n in ((0, 0, 4), (2, 8, 2)):
                link(weighted(buf, h0, n))
                link(weighted(buf + 1, h0 + n, n))
                nc.vector.tensor_tensor(prod[buf][:, 0:n * C], prod[buf][:, 0:n * C], prod[buf + 1][:, 0:n * C],
                                        ALU.add).then_inc(pv_dve, 1)
            dve.wait_ge(sq_done, 1)
            nc.vector.tensor_reduce(ssq[:], sq[:], AX.X, ALU.add).then_inc(var_ready, 1)
            dve.wait_ge(rstd_ready, 4)
            link(nc.vector.tensor_scalar(rms[:], rms[:], 1.0 - LAM_INIT, None, ALU.mult))
            nc.vector.tensor_tensor(o1[:], ps[:, 0, 0:C].rearrange("p (h d) -> p h d", h=NH),
                                    rms[:].unsqueeze(2).broadcast_to([P, NH, HD]), ALU.mult).then_inc(o_ready, 1)
            rest(oT_lo, oT_hi, 1, oT_kept, 2, oT_rest)
            dve.wait_ge(wo_done, 2)
            link(nc.vector.tensor_tensor(x2[:], ps[:, 2, 0:C], x1b[:], ALU.add))
            moments(2, x2[:])
            dve.wait_ge(rstd_ready, 5)
            dve.wait_ge(var_ready, 5)
            nc.vector.tensor_scalar(x2n[:], x2[:], mv[:, 2, 0:1], rstd[:, 2:3], ALU.subtract, ALU.mult).then_inc(xn_ready, 1)
            dve.wait_ge(logit_done, 1)
            link(nc.vector.tensor_copy(lg[:], ps[:, 2, 0:E]))
            link(nc.vector.tensor_reduce(lmax[:], lg[:], AX.X, ALU.max))
            nc.vector.tensor_scalar(lex[:], lg[:], lmax[:, 0:1], None, ALU.subtract).then_inc(lg_ready, 1)
            mine, other = lg[:].unsqueeze(2).broadcast_to([P, E, E]), lg[:].unsqueeze(1).broadcast_to([P, E, E])
            link(nc.vector.tensor_tensor(rk[:], other, mine, ALU.is_gt))
            link(nc.vector.tensor_tensor(rk2[:], other, mine, ALU.is_equal))
            link(nc.vector.tensor_tensor(rk2[:], rk2[:], cs[:, C_TRI:C_ALL].rearrange("p (i j) -> p i j", i=E), ALU.mult))
            link(nc.vector.tensor_tensor(rk[:], rk[:], rk2[:], ALU.add))
            link(nc.vector.tensor_reduce(rank[:], rk[:], AX.X, ALU.add))
            dve.wait_ge(lex_done, 1)
            link(nc.vector.scalar_tensor_tensor(wsel[:], rank[:], 2.0, lex[:], ALU.is_lt, ALU.mult))
            link(nc.vector.tensor_reduce(wsum[:, 0:1], wsel[:], AX.X, ALU.add))
            link(nc.vector.reciprocal(wsum[:, 1:2], wsum[:, 0:1]))
            link(nc.vector.tensor_scalar(wsel[:], wsel[:], wsum[:, 1:2], 0.5, ALU.mult, ALU.mult))

            def hidden(e):
                dve.wait_ge(th_done, e + 1)
                if e >= 2:
                    dve.wait_ge(y_done, e - 1)
                link(nc.vector.scalar_tensor_tensor(hT[:, e % 2, :], th[:, e % 2, :], 1.0, ps[:, 4 + e % 2, :],
                                                    ALU.add, ALU.mult))
                nc.vector.tensor_tensor(hT[:, e % 2, :], hT[:, e % 2, :], ps[:, 6 + e % 2, :], ALU.mult).then_inc(h_done, 1)

            def add_expert(e):
                dve.wait_ge(y_done, e + 1)
                if e >= 1:
                    dve.wait_ge(y_added, e)
                nc.vector.scalar_tensor_tensor(x2[:], ps[:, e % 2, 0:C], wsel[:, e:e + 1], x2[:], ALU.mult,
                                               ALU.add).then_inc(y_added, 1)

            hidden(0)
            for e in range(E):
                if e + 1 < E:
                    hidden(e + 1)
                add_expert(e)


def _turned(w, rows=slice(None)):
    w = np.asarray(w)[rows]
    return np.ascontiguousarray(w.T.reshape(-1, P, w.shape[0]).transpose(1, 0, 2))


def kernel(**inputs):
    import concourse.bacc as _bacc
    from concourse.bass_utils import run_bass_kernel_spmd as _run

    a = {k: np.asarray(v) for k, v in inputs.items()}
    dup = np.repeat(np.arange(NH * HD), 3).reshape(PAIRS, ROWS)
    wq = _turned(a["L0_xattn_wq"])
    wqs = np.zeros((P, KC, PAIRS, KROWS), np.float32)
    wqs[..., :ROWS] = wq[:, :, dup]
    sub = np.arange(C).reshape(NH, D2, 2).transpose(1, 2, 0).reshape(-1)
    wqkv = np.concatenate([_turned(a["L0_attn_Wq"], sub), _turned(a["L0_attn_Wk"], sub), _turned(a["L0_attn_Wv"])], axis=2)
    lams = np.stack([a["L0_attn_lq1"], a["L0_attn_lk1"], a["L0_attn_lq2"], a["L0_attn_lk2"]])
    gu = a["L0_ffn_gate_up_proj"]
    dn = a["L0_ffn_down_proj"]
    arrays = {
        "x": a["x"][0],
        "ctxT": _turned(a["ctx_2048"][0]),
        "mask2": np.broadcast_to(a["mask_BxS2_bk0"], (2, S)),
        "cst": constants(),
        "norm_w": a["L0_xattn_norm_w"].reshape(KC, P).T,
        "wk": _turned(a["L0_xattn_wk"]),
        "wv": _turned(a["L0_xattn_wv"]),
        "wqs": wqs,
        "wg": _turned(a["L0_xattn_wg"]),
        "wo": _turned(a["L0_xattn_wo"]),
        "wqkv": wqkv,
        "wo2": _turned(a["L0_attn_Wo"]),
        "bo": np.broadcast_to(a["L0_attn_bo"], (P, C)),
        "lams": np.broadcast_to(lams, (P, 4, D2)),
        "wr": _turned(a["L0_ffn_gate_weight"]),
        "wgu": np.stack([_turned(gu[e]) for e in range(E)]),
        "wdn": np.stack([_turned(dn[e]) for e in range(E)]),
    }
    nc = _bacc.Bacc("TRN2", target_bir_lowering=False, num_devices=1)
    feed, args = {}, []
    for name, v in arrays.items():
        v = np.ascontiguousarray(v)
        feed[f"in_{name}"] = v
        args.append(nc.dram_tensor(f"in_{name}", v.shape, mybir.dt.from_np(v.dtype), kind="ExternalInput").ap())
    out = nc.dram_tensor("out_0", (T, C), F32, kind="ExternalOutput").ap()
    perceiver_layer(nc, *args, out)
    r = _run(nc, [feed], core_ids=[0])
    return r.results[0]["out_0"].reshape(1, T, C)
```

```python
from contextlib import ExitStack

import numpy as np

import concourse.bass as bass
from concourse import mybir

F32 = mybir.dt.float32
F32R = mybir.dt.float32r
U8 = mybir.dt.uint8
ALU = mybir.AluOpType
ACT = mybir.ActivationFunctionType
AX = mybir.AxisListType

P = 128
T = 128
C = 256
KC = C // P
S = 2048
NH, HD = 16, 16
PAIRS = NH // 2
ROWS = 2 * HD * 3
ONES_ROW, MASK_ROW = ROWS, ROWS + 1
KROWS = ROWS + 2
BANK = 512
KCH = S // BANK
KB = S // P
HALF = 2 * BANK
NPIECE = NH * S // HALF
CHUNKS = PAIRS * KB // 2
PT = 4
VW = 32
D2 = HD // 2
SUB = 2 * NH
E, I = 8, 512
IC = I // P
GU_SPLIT = 384
MASKED = -float(2.0 ** 100)
FLOOR = -float(2.0 ** 96)
FMAX = 3.4028234663852886e38
LAM_INIT = 0.8 - 0.6 * float(np.exp(-0.3 * 12))
LN_EPS, RMS_EPS = 1e-5, 1e-6

C_M0, C_M1, C_S0, C_S1, C_KS, C_KB, C_EPS, C_POW = range(8)
C_ID = 8
C_NEG = C_ID + P
C_SEL = C_NEG + P
C_TRI = C_SEL + 64
C_ALL = C_TRI + E * E


def constants():
    c = np.zeros((P, C_ALL), np.float32)
    r = np.arange(ROWS)
    scale = HD ** -0.5
    for j in range(2):
        own = (r % (2 * HD)) // HD == j
        c[:ROWS, C_M0 + j] = own * scale
        c[:ROWS, C_S0 + j] = (own & (r // (2 * HD) == 1)) * -scale
    c[ONES_ROW, C_KS], c[ONES_ROW, C_KB] = 0.0, 1.0
    c[MASK_ROW, C_KS], c[MASK_ROW, C_KB] = -MASKED, MASKED
    c[:, C_POW] = -0.5
    c[:, C_EPS] = LN_EPS / (1.0 - LAM_INIT) ** 2
    c[:, C_ID:C_ID + P] = np.eye(P)
    c[:, C_NEG:C_NEG + P] = -np.eye(P)
    q = np.arange(P)
    c[q, C_SEL + 32 * (q // 64) + q % 32] = 1.0
    c[:, C_TRI:C_TRI + E * E] = np.tril(np.ones((E, E)), -1).reshape(-1)
    return c


def perceiver_layer(nc, x, ctxT, mask2, cst, norm_w, wk, wv, wqg, wo, wqkv, wo2, bo, lams, wr, wgu, wdn, out):
    with ExitStack() as ctx:
        def sb(name, shape, dt=F32):
            return ctx.enter_context(nc.sbuf_tensor(name, shape, dt))

        def sem(name):
            return ctx.enter_context(nc.semaphore(name))

        base = (nc.sbuf_base + 63) // 64 * 64
        KIB = 1024
        arena = sb("arena", [P, 151 * KIB // 4 + 16])

        def at(name, shape, kib, dt=F32):
            return nc.alloc_sbuf_tensor_at(name, shape, dt, offset=base + kib * KIB)

        kstack = [at("kstack_a", [P, 4, S], 0, F32R), at("kstack_b", [P, 4, S], 32, F32R)]
        ctx_hi = at("ctx_hi", [P, KC, S], 32, F32R)
        ctx_lo = at("ctx_lo", [P, KC, S], 48, F32R)
        vals = at("vals", [P, KB, NH, VW], 64)
        ctx_raw = at("ctx_raw", [P, KC, S], 64)
        k_hi = at("k_hi", [P, 2, S], 96, F32R)
        k_lo = at("k_lo", [P, 2, S], 112, F32R)
        probs = at("probs", [P, PT, BANK], 128)
        qneg = at("qneg", [KROWS, 2, PAIRS, T], 128, F32R)
        qstack = at("qstack", [P, PAIRS, 2, T], 136, F32R)
        w_at = [96, 108, 0, 12, 32, 44, 64, 76]
        gu_w = [at(f"gate_up{e}", [P, KC, 2 * I], w_at[e]) for e in range(E)]
        dn_w = [at(f"down{e}", [P, IC, C], w_at[e] + 8) for e in range(E)]
        prod = [at(f"prod{i}", [P, 1024], kib) for i, kib in enumerate([24, 28, 56, 60, 88, 92, 120, 124])]
        shifted = at("shifted", [P, SUB, SUB], 128)
        q_tok = at("q_tok", [T, PAIRS, 3, 2 * HD], 148)
        wqg_s = at("wqg_s", [P, KC, 2 * C], 144)
        wqkv_hi, wqkv_lo = at("wqkv_hi", [P, KC, 3 * C], 120, F32R), at("wqkv_lo", [P, KC, 3 * C], 144, F32R)
        th = at("th", [P, 2, I], 24)
        h_hi, h_lo = at("h_hi", [P, 2, I], 28, F32R), at("h_lo", [P, 2, I], 144, F32R)
        gu_hi = [at(f"gate_up_hi{i}", [P, KC, 2 * I], kib, F32R) for i, kib in enumerate([88, 120, 56])]
        pv_pool_prod = [at(f"pv_prod{i}", [P, 2 * C], kib) for i, kib in enumerate([144, 146])]
        gu_lo = [at(f"gate_up_lo{e}", [P, KC, 2 * I], w_at[e], F32R) for e in range(E)]
        dn_hi_kib = [136 + 4 * (e % 2) for e in range(E - 1)] + [56]
        dn_lo_kib = [132 - 4 * (e % 2) for e in range(E - 1)] + [60]
        dn_hi = [at(f"down_hi{e}", [P, IC, C], dn_hi_kib[e], F32R) for e in range(E)]
        dn_lo = [at(f"down_lo{e}", [P, IC, C], dn_lo_kib[e], F32R) for e in range(E)]

        cs = sb("cs", [P, C_ALL])
        ident, nident = cs[:, C_ID:C_ID + P], cs[:, C_NEG:C_NEG + P]
        nw = sb("nw", [P, KC])
        xs = sb("xs", [P, C])
        mask_u8 = sb("mask_u8", [P, S], U8)
        wk_s, wk_hi, wk_lo = sb("wk_s", [P, KC, C]), sb("wk_hi", [P, KC, C], F32R), sb("wk_lo", [P, KC, C], F32R)
        wv_s, wv_hi, wv_lo = sb("wv_s", [P, KC, C]), sb("wv_hi", [P, KC, C], F32R), sb("wv_lo", [P, KC, C], F32R)
        wo_s, wo2_s = sb("wo_s", [P, KC, C]), sb("wo2_s", [P, KC, C])
        wqkv_s = sb("wqkv_s", [P, KC, 3 * C])
        bo_s, lam_s, wr_s = sb("bo_s", [P, C]), sb("lam_s", [P, 4, D2]), sb("wr_s", [P, KC, E])
        warm_out = sb("warm_out", [P, 1])
        warm = sb("warm", [P, P])
        stat, mv, rstd, ms = sb("stat", [P, 3, 6]), sb("mv", [P, 3, 2]), sb("rstd", [P, 3]), sb("ms", [P, 2])
        junk, hn, h2 = sb("junk", [P, C]), sb("hn", [P, C]), sb("h2", [P, C])
        xnT = sb("xnT", [P, KC, T])
        gate = sb("gate", [P, C])
        part_max, row_max = sb("part_max", [P, NPIECE]), sb("row_max", [P, NH])
        acc_s = sb("acc_s", [P, PAIRS, T])
        den, rden = sb("den", [P, NH]), sb("rden", [P, NH])
        wo_hi, wo_lo, wo2_hi, wo2_lo = wk_hi, wk_lo, wv_hi, wv_lo
        o1 = sb("o1", [P, NH, HD])
        o1f = o1[:].rearrange("p h d -> p (h d)")
        oT_hi, oT_lo = sb("oT_hi", [P, KC, T], F32R), sb("oT_lo", [P, KC, T], F32R)
        x1, x1b = sb("x1", [P, C]), sb("x1b", [P, C])
        x1T_hi, x1T_lo = sb("x1T_hi", [P, KC, T], F32R), sb("x1T_lo", [P, KC, T], F32R)
        qd, kd, vd = sb("qd", [P, D2, SUB]), sb("kd", [P, D2, SUB]), sb("vd", [P, NH, HD])
        smax, ssum, srec = sb("smax", [P, SUB]), sb("ssum", [P, SUB]), sb("srec", [P, SUB])
        dif, dif1 = sb("dif", [P, NH, NH]), sb("dif1", [P, NH, NH])
        lsum, lexp, nlam = sb("lsum", [P, 2]), sb("lexp", [P, 2]), sb("nlam", [P, 1])
        sq, ssq, rms = sb("sq", [P, NH, HD]), sb("ssq", [P, NH]), sb("rms", [P, NH])
        x2 = sb("x2", [P, C])
        x2T_hi, x2T_lo = x1T_hi, x1T_lo
        x1n = x2n = h2
        lg, rk, rk2 = sb("lg", [P, E]), sb("rk", [P, E, E]), sb("rk2", [P, E, E])
        rank, lmax, lex, wsel, wsum = sb("rank", [P, E]), sb("lmax", [P, 1]), sb("lex", [P, E]), sb("wsel", [P, E]), sb("wsum", [P, 2])

        ps = ctx.enter_context(nc.psum_tensor("ps", [P, 8, BANK], F32))

        ld = {n: sem("loaded_" + n) for n in
              ("x", "cst", "wk", "wv", "wqg", "nw", "mask", "wo", "wqkv", "wo2", "small")}
        ld_ctx = [sem(f"loaded_ctx{i}") for i in range(KCH)]
        ld_exp = [sem(f"loaded_expert{e}") for e in range(E)]
        kst_loaded = [sem(f"kstack_loaded{p}") for p in range(PAIRS)]
        out_saved = sem("out_saved")
        vchain, achain, pchain = sem("vector_chain"), sem("scalar_chain"), sem("pool_chain")
        warm_in = sem("warm_in")
        wk_split, wv_split = sem("wk_split"), sem("wv_split")
        ctx_hi_done, ctx_lo_done = sem("ctx_hi_done"), sem("ctx_lo_done")
        kproj, k_hi_done, k_lo_done = sem("k_projected"), sem("k_hi_done"), sem("k_lo_done")
        vproj, v_kept = sem("v_projected"), sem("v_kept")
        v_pads = sem("v_pads")
        kst_const = sem("kstack_constant_rows")
        var_ready, rstd_ready = sem("variance_ready"), sem("rstd_ready")
        xn_ready, xT_ready, xT_kept = sem("xn_ready"), sem("xT_ready"), sem("xT_kept")
        qg_proj, q_kept, q_rows = sem("query_gate_projected"), sem("q_kept"), sem("q_constant_rows")
        q_tok_kept, q_turned, g_kept = sem("q_of_tokens_kept"), sem("q_turned"), sem("gate_kept")
        piece, piece_max, rowmax = sem("piece_scored"), sem("piece_max"), sem("row_max_ready")
        mx_turned, mx_kept = sem("max_turned"), sem("max_kept")
        scored, expd, weighed = sem("chunk_scored"), sem("chunk_exp"), sem("chunk_weighed")
        acc_kept, z_ready, o_ready = sem("acc_kept"), sem("z_ready"), sem("o_ready")
        oT_ready, oT_kept, wo_done = sem("oT_ready"), sem("oT_kept"), sem("wo_done")
        qkv_done, q2_kept, v2_kept = sem("qkv_done"), sem("q2_kept"), sem("v2_kept")
        k2_kept = sem("k2_kept")
        w_split = sem("late_weights_split")
        oT_rest, x1T_rest = sem("oT_rest_kept"), sem("x1T_rest_kept")
        lam_in, lam_exp = sem("lambda_in"), sem("lambda_exp")
        dve_part, pool_part, s_done = sem("score_part_vector"), sem("score_part_pool"), sem("scores_done")
        shifted_ready, sexp = sem("shifted_ready"), sem("scores_exp")
        dif_ready, pv_dve, pv_pool, pv_done = sem("diff_ready"), sem("pv_part_vector"), sem("pv_part_pool"), sem("pv_done")
        root_kept = sem("root_kept")
        sq_done = sem("square_done")
        logit_done, lg_ready, lex_done = sem("logits_done"), sem("logits_ready"), sem("logits_exp")
        gu_done, th_done = sem("gate_up_done"), sem("tanh_done")
        h_done, h_turned, x2T_rest = sem("hidden_done"), sem("hidden_turned"), sem("x2T_rest_kept")
        gu_hi_done, gu_lo_pool, gu_lo_dve = sem("gate_up_hi_done"), sem("gate_up_lo_pool"), sem("gate_up_lo_vector")
        h_hi_done, h_lo_done = sem("hidden_hi_done"), sem("hidden_lo_done")
        dn_hi_done, dn_lo_done = sem("down_hi_done"), sem("down_lo_done")
        y_done, out_ready = sem("down_done"), sem("out_ready")

        block = ctx.enter_context(nc.Block())

        def acc_place(p):
            return (2, slice(0, T)) if p == PAIRS - 1 else (6 + p // 4, slice((p % 4) * T, (p % 4 + 1) * T))

        def max_bank(p):
            return 7 if p <= PAIRS // 2 else 6

        def stack(p):
            return kstack[p // 4][:, p % 4, :]

        @block.sync
        def _(sp):
            def load(dst, src, name):
                sp.dma_start(dst, src).then_inc(ld[name], 16)

            def load_context(i):
                sl = slice(i * BANK, (i + 1) * BANK)
                sp.dma_start(ctx_raw[:, :, sl], ctxT[:, :, sl]).then_inc(ld_ctx[i], 16)

            load(wk_s[:], wk, "wk")
            load_context(0)
            load_context(1)
            load_context(2)
            load(mask_u8[ONES_ROW:MASK_ROW + 1, :], mask2, "mask")
            load(xs[:], x, "x")
            load(cs[:], cst, "cst")
            load_context(3)
            load(nw[:], norm_w, "nw")
            load(wv_s[:], wv, "wv")
            load(wqg_s[:], wqg, "wqg")

            def load_stack(p):
                m, own = p // 4, slice(32 * (p % 4), 32 * (p % 4) + 32)
                for part, tile in enumerate((k_hi, k_hi, k_lo)):
                    sp.dma_start(stack(p)[32 * part:32 * part + 32].bitcast(F32),
                                 tile[own, m, :].bitcast(F32)).then_inc(kst_loaded[p], 16)

            sp.wait_ge(k_hi_done, KCH)
            sp.wait_ge(k_lo_done, KCH)
            load_stack(0)
            load_stack(1)
            for dst, src in ((bo_s, bo), (lam_s, lams), (wr_s, wr)):
                load(dst[:], src, "small")
            load_stack(2)
            load_stack(3)
            sp.wait_ge(k_hi_done, 2 * KCH)
            sp.wait_ge(k_lo_done, 2 * KCH)
            sp.wait_ge(vproj, KB)
            for p in range(4, PAIRS):
                load_stack(p)
            sp.dma_start(wo_s[:], wo).then_inc(ld["wo"], 16)
            sp.dma_start(wqkv_s[:], wqkv).then_inc(ld["wqkv"], 16)
            sp.dma_start(wo2_s[:], wo2).then_inc(ld["wo2"], 16)

            def load_expert(e):
                sp.dma_start(gu_w[e][:], wgu[e]).then_inc(ld_exp[e], 16)
                sp.dma_start(dn_w[e][:], wdn[e]).then_inc(ld_exp[e], 16)

            for p in range(PAIRS):
                sp.wait_ge(kst_loaded[p], 48)
            load_expert(0)
            load_expert(1)
            sp.wait_ge(scored, CHUNKS // 2)
            load_expert(2)
            load_expert(3)
            sp.wait_ge(scored, CHUNKS)
            load_expert(4)
            load_expert(5)
            sp.wait_ge(weighed, CHUNKS)
            load_expert(6)
            load_expert(7)
            sp.wait_ge(out_ready, 1)
            sp.dma_start(out, x2[:]).then_inc(out_saved, 16)
            sp.wait_ge(out_saved, 16)

        @block.scalar
        def _(act):
            act.wait_ge(warm_in, 1)
            nc.scalar.activation(warm_out[:], warm[:, 0:1], ACT.Copy).then_inc(achain, 1)

            def context_hi(i):
                sl = slice(i * BANK, (i + 1) * BANK)
                act.wait_ge(ld_ctx[i], 16)
                for kc in range(KC):
                    nc.scalar.activation(ctx_hi[:, kc, sl], ctx_raw[:, kc, sl], ACT.Copy).then_inc(ctx_hi_done, 1)

            def key_hi(i):
                m, ch = divmod(i, KCH)
                act.wait_ge(kproj, i + 1)
                nc.scalar.activation(k_hi[:, m, ch * BANK:(ch + 1) * BANK], ps[:, i % 4, :],
                                     ACT.Copy).then_inc(k_hi_done, 1)

            context_hi(0)
            context_hi(1)
            for i in range(2 * KCH):
                if i + 2 < KCH:
                    context_hi(i + 2)
                key_hi(i)
                if i == 6:
                    act.wait_ge(qg_proj, 1)
                    nc.scalar.activation(q_tok[:], ps[:, 5, 0:C].rearrange("t (p r) -> t p r", p=PAIRS).unsqueeze(2)
                                         .broadcast_to([T, PAIRS, 3, 2 * HD]),
                                         ACT.Copy).then_inc(q_tok_kept, 1)
                    nc.scalar.activation(gate[:], ps[:, 5, C:2 * C], ACT.Tanh, scale=0.5).then_inc(g_kept, 1)
            def keep_max(p):
                act.wait_ge(mx_turned, p + 1)
                nc.scalar.activation(qstack[ONES_ROW:ONES_ROW + 1, p, :, :],
                                     ps[ONES_ROW:ONES_ROW + 1, max_bank(p), 0:2 * T].rearrange("o (j t) -> o j t", j=2),
                                     ACT.Copy).then_inc(mx_kept, 1)

            act.wait_ge(ctx_lo_done, KC * KCH)
            act.wait_ge(ctx_hi_done, KC * KCH)
            for kb in range(KB):
                if kb == KB - 1:
                    keep_max(0)
                act.wait_ge(vproj, kb + 1)
                nc.scalar.activation(vals[:, kb, :, 0:HD],
                                     ps[:, 4 + kb % 2, 0:C].rearrange("p (h d) -> p h d", h=NH),
                                     ACT.Copy).then_inc(v_kept, 1)

            def keep_heads(half):
                act.wait_ge(oT_ready, half + 1)
                nc.scalar.activation(oT_hi[:, half, :], ps[:, 3, half * T:(half + 1) * T], ACT.Copy).then_inc(oT_kept, 1)

            for g in range(CHUNKS):
                if g == CHUNKS - 2:
                    keep_heads(0)
                act.wait_ge(scored, g + 1)
                if g >= PT:
                    act.wait_ge(weighed, g - PT + 1)
                nc.scalar.activation(probs[:, g % PT, :], ps[:, 4 + g % 2, :], ACT.Exp).then_inc(expd, 1)
                if g % 8 == 5 and g // 8 + 1 < PAIRS:
                    keep_max(g // 8 + 1)
            act.wait_ge(lam_in, 2)
            nc.scalar.activation(lexp[:], lsum[:], ACT.Exp).then_inc(lam_exp, 1)
            keep_heads(1)
            act.wait_ge(xT_ready, 2)
            nc.scalar.activation(x1T_hi[:], ps[:, 3, 0:C].rearrange("p (c t) -> p c t", c=KC), ACT.Copy).then_inc(xT_kept, 1)
            act.wait_ge(qkv_done, 1)
            nc.scalar.activation(qd[:], ps[:, 4, 0:C].rearrange("p (d s) -> p d s", d=D2), ACT.Copy,
                                 scale=D2 ** -0.5).then_inc(q2_kept, 1)
            act.wait_ge(qkv_done, 3)
            nc.scalar.activation(vd[:], ps[:, 1, 0:C].rearrange("p (h d) -> p h d", h=NH), ACT.Copy).then_inc(v2_kept, 1)
            for half in range(2):
                act.wait_ge(shifted_ready, half + 1)
                rows = slice(half * NH, (half + 1) * NH)
                nc.scalar.activation(shifted[:, rows, :], shifted[:, rows, :], ACT.Exp).then_inc(sexp, 1)
            act.wait_ge(achain, 1)
            nc.scalar.activation(warm_out[:], warm[:, 0:1], ACT.Sqrt).then_inc(achain, 1)

            def down_hi(e):
                act.wait_ge(ld_exp[e], 32)
                if e == E - 1:
                    act.wait_ge(gu_done, E - 2)
                elif e >= 2:
                    act.wait_ge(y_done, e - 1)
                nc.scalar.activation(dn_hi[e][:], dn_w[e][:], ACT.Copy).then_inc(dn_hi_done, 1)

            def gate_up_hi(e):
                act.wait_ge(ld_exp[e], 32)
                if e >= 3:
                    act.wait_ge(gu_done, e - 2)
                for kc in range(KC):
                    nc.scalar.activation(gu_hi[e % 3][:, kc, :], gu_w[e][:, kc, :], ACT.Copy).then_inc(gu_hi_done, 1)

            act.wait_ge(s_done, 2)
            gate_up_hi(0)
            gate_up_hi(1)
            down_hi(0)
            down_hi(1)
            act.wait_ge(pv_done, 1)
            nc.scalar.activation(sq[:], ps[:, 0, 0:C].rearrange("p (h d) -> p h d", h=NH), ACT.Square).then_inc(sq_done, 1)
            act.wait_ge(var_ready, 4)
            nc.scalar.activation(rms[:], ssq[:], ACT.Sqrt, bias=cs[:, C_EPS:C_EPS + 1],
                                 scale=1.0 / (HD * (1.0 - LAM_INIT) ** 2)).then_inc(root_kept, 1)
            act.wait_ge(oT_ready, 3)
            nc.scalar.activation(oT_hi[:], ps[:, 1, 0:C].rearrange("p (c t) -> p c t", c=KC), ACT.Copy).then_inc(oT_kept, 1)
            act.wait_ge(achain, 2)
            nc.scalar.activation(warm_out[:], warm[:, 0:1], ACT.Exp).then_inc(achain, 1)
            gate_up_hi(2)
            act.wait_ge(xT_ready, 3)
            nc.scalar.activation(x2T_hi[:], ps[:, 3, 0:C].rearrange("p (c t) -> p c t", c=KC), ACT.Copy).then_inc(xT_kept, 1)
            act.wait_ge(lg_ready, 1)
            nc.scalar.activation(lex[:], lex[:], ACT.Exp).then_inc(lex_done, 1)

            def tanh(e):
                act.wait_ge(gu_done, e + 1)
                if e >= 2:
                    act.wait_ge(h_turned, e - 1)
                nc.scalar.activation(th[:, e % 2, :], ps[:, 4 + e % 2, :], ACT.Tanh, scale=0.5).then_inc(th_done, 1)

            def hidden_hi(e):
                act.wait_ge(h_turned, e + 1)
                if e >= 2:
                    act.wait_ge(y_done, e - 1)
                nc.scalar.activation(h_hi[:, e % 2, :], ps[:, 2 + e % 2, :], ACT.Copy).then_inc(h_hi_done, 1)

            tanh(0)
            for e in range(E):
                if e + 1 < E:
                    tanh(e + 1)
                hidden_hi(e)
                if e + 3 < E:
                    gate_up_hi(e + 3)
                if 2 <= e + 1 < E - 1:
                    down_hi(e + 1)
                if e + 2 == E - 1:
                    down_hi(E - 1)

        @block.gpsimd
        def _(pool):
            chain = [0]

            def link(ins):
                chain[0] += 1
                ins.then_inc(pchain, 1)
                pool.wait_ge(pchain, chain[0])

            nc.gpsimd.memset(warm[:], 0.0).then_inc(warm_in, 1)
            pool.wait_ge(warm_in, 1)
            rows = qstack[ONES_ROW:KROWS, :, :, :].bitcast(F32)
            link(nc.gpsimd.memset(rows, 1.0))
            nc.gpsimd.memset(qstack[ONES_ROW:ONES_ROW + 1, :, :, :].bitcast(F32), 0.0).then_inc(q_rows, 1)
            pool.wait_ge(q_rows, 1)

            def root(col, src, eps):
                link(nc.gpsimd.tensor_scalar(rstd[:, col:col + 1], src, 1.0, eps, ALU.mult, ALU.add))
                nc.gpsimd.tensor_tensor(rstd[:, col:col + 1], rstd[:, col:col + 1], cs[:, C_POW:C_POW + 1],
                                        ALU.pow).then_inc(rstd_ready, 1)

            def const_rows(p):
                r = slice(ONES_ROW, KROWS)
                nc.gpsimd.tensor_scalar(stack(p)[r], mask_u8[r, :], cs[r, C_KS:C_KS + 1], cs[r, C_KB:C_KB + 1],
                                        ALU.mult, ALU.add).then_inc(kst_const, 1)
                pool.wait_ge(kst_const, p + 1)

            pool.wait_ge(ld["mask"], 16)
            pool.wait_ge(ld["cst"], 16)
            const_rows(0)
            pool.wait_ge(var_ready, 1)
            root(0, mv[:, 0, 1:2], LN_EPS)
            pool.wait_ge(var_ready, 2)
            pool.wait_ge(rstd_ready, 1)
            root(0, ms[:, 0:1], RMS_EPS)
            pool.wait_ge(rstd_ready, 2)
            pool.wait_ge(ld["wv"], 16)
            link(nc.gpsimd.tensor_copy(wv_hi[:], wv_s[:]))
            nc.gpsimd.tensor_tensor(wv_lo[:], wv_s[:], wv_hi[:].bitcast(F32), ALU.subtract).then_inc(wv_split, 1)
            pool.wait_ge(wv_split, 1)
            pool.wait_ge(ctx_lo_done, KC * KCH)
            pool.wait_ge(ctx_hi_done, KC * KCH)
            nc.gpsimd.memset(vals[:, :, :, HD:HD + 1], 1.0).then_inc(v_pads, 1)
            nc.gpsimd.memset(vals[:, :, :, HD + 1:VW], 0.0).then_inc(v_pads, 1)
            pool.wait_ge(v_pads, 2)
            for p in range(1, 4):
                const_rows(p)
            pool.wait_ge(vproj, KB)
            for p in range(4, PAIRS):
                const_rows(p)

            for p in range(PAIRS):
                pool.wait_ge(kst_loaded[p], 48)
            for name, w, hi, lo in (("wo", wo_s, wo_hi[:], wo_lo[:]), ("wqkv", wqkv_s, wqkv_hi[:], wqkv_lo[:]),
                                    ("wo2", wo2_s, wo2_hi[:], wo2_lo[:])):
                pool.wait_ge(ld[name], 16)
                link(nc.gpsimd.tensor_copy(hi, w[:]))
                nc.gpsimd.tensor_tensor(lo, w[:], hi.bitcast(F32), ALU.subtract).then_inc(w_split, 1)

            pool.wait_ge(w_split, 3)
            pool.wait_ge(var_ready, 3)
            root(1, mv[:, 1, 1:2], LN_EPS)
            pool.wait_ge(q2_kept, 1)
            pool.wait_ge(k2_kept, 1)
            pool.wait_ge(weighed, CHUNKS)

            def product(half, d):
                rows = slice(half * NH, (half + 1) * NH)
                return nc.gpsimd.tensor_tensor(prod[d][:, half * BANK:(half + 1) * BANK].rearrange("p (a b) -> p a b", a=NH),
                                               qd[:, d, rows].unsqueeze(2).broadcast_to([P, NH, SUB]),
                                               kd[:, d, :].unsqueeze(1).broadcast_to([P, NH, SUB]), ALU.mult)

            pool.wait_ge(qkv_done, 3)
            for half in range(2):
                cols = slice(half * BANK, (half + 1) * BANK)
                product(half, 5).then_inc(pool_part, 1)
                if half == 1:
                    link(product(half, 6))
                    link(product(half, 7))
                    nc.gpsimd.tensor_tensor(prod[6][:, cols], prod[6][:, cols], prod[7][:, cols],
                                            ALU.add).then_inc(pool_part, 1)
                else:
                    product(half, 6).then_inc(pool_part, 1)
                    product(half, 7).then_inc(pool_part, 1)
            pool.wait_ge(dif_ready, 1)
            pool.wait_ge(s_done, 2)
            pool.wait_ge(v2_kept, 1)
            link(nc.gpsimd.tensor_tensor(
                pv_pool_prod[0][:].rearrange("p (h a d) -> p h a d", h=2, a=NH),
                dif[:, :, 12:14].rearrange("p a h -> p h a").unsqueeze(3).broadcast_to([P, 2, NH, HD]),
                vd[:, 12:14, :].unsqueeze(2).broadcast_to([P, 2, NH, HD]), ALU.mult))
            link(nc.gpsimd.tensor_tensor(
                pv_pool_prod[1][:].rearrange("p (h a d) -> p h a d", h=2, a=NH),
                dif[:, :, 14:16].rearrange("p a h -> p h a").unsqueeze(3).broadcast_to([P, 2, NH, HD]),
                vd[:, 14:16, :].unsqueeze(2).broadcast_to([P, 2, NH, HD]), ALU.mult))
            nc.gpsimd.tensor_tensor(pv_pool_prod[0][:], pv_pool_prod[0][:], pv_pool_prod[1][:],
                                    ALU.add).then_inc(pv_pool, 1)

            def down_lo(e):
                pool.wait_ge(dn_hi_done, e + 1)
                if e == E - 1:
                    pool.wait_ge(gu_done, E - 2)
                elif e >= 2:
                    pool.wait_ge(y_done, e - 1)
                nc.gpsimd.tensor_tensor(dn_lo[e][:], dn_w[e][:], dn_hi[e][:].bitcast(F32),
                                        ALU.subtract).then_inc(dn_lo_done, 1)

            def gate_up_lo(e):
                pool.wait_ge(gu_hi_done, KC * (e + 1))
                nc.gpsimd.tensor_tensor(gu_lo[e][:, 1, GU_SPLIT:], gu_w[e][:, 1, GU_SPLIT:],
                                        gu_hi[e % 3][:, 1, GU_SPLIT:].bitcast(F32), ALU.subtract).then_inc(gu_lo_pool, 1)

            gate_up_lo(0)
            gate_up_lo(1)
            down_lo(0)
            pool.wait_ge(var_ready, 5)
            root(2, mv[:, 2, 1:2], LN_EPS)
            down_lo(1)
            gate_up_lo(2)
            for e in range(2, E):
                if e + 1 < E:
                    gate_up_lo(e + 1)
                if e >= 3:
                    down_lo(e - 1)
            down_lo(E - 1)

        @block.tensor
        def _(pe):
            def split_product(dst, a_hi, a_lo, b_hi, b_lo, ready=lambda n, kc: None):
                for n, (a, b) in enumerate(((a_hi, b_hi), (a_lo, b_hi), (a_hi, b_lo))):
                    for kc in range(KC):
                        ready(n, kc)
                        last = nc.tensor.matmul(dst, a(kc), b(kc), start=(kc == 0 and n == 0),
                                                stop=(kc == KC - 1 and n == 2))
                return last

            def key_projection(i):
                m, ch = divmod(i, KCH)

                def ready(n, kc):
                    if m == 0 and n == 0:
                        pe.wait_ge(ctx_hi_done, KC * ch + kc + 1)
                    if m == 0 and n == 2:
                        pe.wait_ge(ctx_lo_done, KC * ch + kc + 1)
                    if i == 0 and n == 1 and kc == 0:
                        pe.wait_ge(wk_split, 2)

                if i >= 4:
                    pe.wait_ge(k_hi_done, i - 3)
                    pe.wait_ge(k_lo_done, i - 3)
                rows, keys = slice(m * P, (m + 1) * P), slice(ch * BANK, (ch + 1) * BANK)
                split_product(ps[:, i % 4, :],
                              lambda kc: wk_hi[:, kc, rows], lambda kc: wk_lo[:, kc, rows],
                              lambda kc: ctx_hi[:, kc, keys], lambda kc: ctx_lo[:, kc, keys],
                              ready).then_inc(kproj, 1)

            def value_projection(kb):
                if kb == 0:
                    pe.wait_ge(wv_split, 1)
                if kb == 1:
                    pe.wait_ge(g_kept, 1)
                if kb >= 2:
                    pe.wait_ge(v_kept, kb - 1)
                keys = slice(kb * P, (kb + 1) * P)
                split_product(ps[:, 4 + kb % 2, 0:C],
                              lambda kc: ctx_hi[:, kc, keys], lambda kc: ctx_lo[:, kc, keys],
                              lambda kc: wv_hi[:, kc, :], lambda kc: wv_lo[:, kc, :]).then_inc(vproj, 1)

            def turn(bank, src):
                for kc in range(KC):
                    last = nc.tensor.transpose(ps[:, bank, kc * T:(kc + 1) * T], src[:, kc * P:(kc + 1) * P], ident)
                return last

            def project(dst, lhs, w, cols):
                for kc in range(KC):
                    last = nc.tensor.matmul(dst, lhs[:, kc, :], w[:, kc, cols], start=(kc == 0), stop=(kc == KC - 1))
                return last

            def project_split(dst, hi, lo, w_hi, w_lo, cols):
                return split_product(dst, lambda kc: hi[:, kc, :], lambda kc: lo[:, kc, :],
                                     lambda kc: w_hi[:, kc, cols], lambda kc: w_lo[:, kc, cols])

            def keep_clock(n, bank=0, a=ident):
                for _ in range(n):
                    nc.tensor.matmul(ps[:, bank, 0:P], a, a, start=True, stop=True)

            def max_piece(a):
                h, half = divmod(a, 2)
                p, j = divmod(h, 2)
                if a % 4 == 0:
                    pe.wait_ge(kst_loaded[p], 48)
                    pe.wait_ge(kst_const, p + 1)
                if a == NPIECE // 2:
                    pe.wait_ge(q_kept, 4)
                if a == 0:
                    pe.wait_ge(q_rows, 1)
                    pe.wait_ge(q_kept, 2)
                    pe.wait_ge(k_hi_done, 2 * KCH)
                    pe.wait_ge(k_lo_done, 2 * KCH)
                if a >= 2:
                    pe.wait_ge(piece_max, a - 1)
                for n in range(2):
                    keys = slice(half * HALF + n * BANK, half * HALF + (n + 1) * BANK)
                    last = nc.tensor.matmul(ps[:, 2 * (a % 2) + n, :], qstack[0:KROWS, p, j, :], stack(p)[0:KROWS, keys],
                                            start=True, stop=True)
                last.then_inc(piece, 1)

            def turn_max(p):
                pe.wait_ge(rowmax, 2 * p + 2)
                if p >= 5:
                    pe.wait_ge(acc_kept, 1)
                for j in range(2):
                    last = nc.tensor.matmul(ps[ONES_ROW:ONES_ROW + 1, max_bank(p), j * T:(j + 1) * T],
                                            row_max[:, 2 * p + j:2 * p + j + 1], nident, start=True, stop=True)
                last.then_inc(mx_turned, 1)

            def score(g):
                p, c = divmod(g, KB // 2)
                if g < 2:
                    pe.wait_ge(v_kept, KB)
                if g >= 2:
                    pe.wait_ge(expd, g - 1)
                if c == 0:
                    pe.wait_ge(mx_kept, p + 1)
                for n in range(2):
                    kb = 2 * c + n
                    last = nc.tensor.matmul(ps[:, 4 + g % 2, n * 2 * T:(n + 1) * 2 * T],
                                            stack(p)[0:KROWS, kb * P:(kb + 1) * P], qstack[0:KROWS, p, :, :],
                                            start=True, stop=True)
                last.then_inc(scored, 1)

            def weigh(g):
                p, c = divmod(g, KB // 2)
                pe.wait_ge(expd, g + 1)
                if g == 0:
                    pe.wait_ge(v_pads, 2)
                for n in range(2):
                    kb = 2 * c + n
                    for j in range(2):
                        row = 32 * (2 * j + n)
                        last = nc.tensor.matmul(ps[row:row + VW, *acc_place(p)],
                                                vals[:, kb, 2 * p + j, :], probs[:, g % PT, (2 * n + j) * T:(2 * n + j + 1) * T],
                                                start=(c == 0), stop=(c == KB // 2 - 1), skip_group_check=True)
                last.then_inc(weighed, 1)

            pe.wait_ge(warm_in, 1)
            keep_clock(11, 7, warm[:])
            pe.wait_ge(wk_split, 1)
            for i in range(5):
                key_projection(i)
            pe.wait_ge(xn_ready, 1)
            pe.wait_ge(ld["cst"], 16)
            turn(7, h2).then_inc(xT_ready, 1)
            key_projection(5)
            key_projection(6)
            pe.wait_ge(xT_kept, 1)
            pe.wait_ge(ld["wqg"], 16)
            project(ps[:, 5, :], xnT, wqg_s, slice(0, 2 * C)).then_inc(qg_proj, 1)
            key_projection(7)
            pe.wait_ge(q_tok_kept, 1)
            for p in range(PAIRS):
                mine = q_tok[:, p].rearrange("t b r -> t (b r)")
                last = nc.tensor.matmul(ps[0:ROWS, 6 + p // 4, (p % 4) * T:(p % 4 + 1) * T], mine, ident,
                                        start=True, stop=True)
                if p % 4 == 3:
                    last.then_inc(q_turned, 1)
            first_pieces = {6: 0, 8: 1, 9: 2, 11: 3, 12: 4, 14: 5}
            for kb in range(KB):
                value_projection(kb)
                if kb == 14:
                    turn_max(0)
                if kb in first_pieces:
                    max_piece(first_pieces[kb])

            def sum_keys(first, end):
                for p in range(first, end):
                    last = nc.tensor.matmul(ps[:, p // 4, p % 4 * 64:(p % 4 + 1) * 64], acc_s[:, p, :],
                                            cs[:, C_SEL:C_SEL + 64], start=True, stop=True)
                return last

            def turn_heads(half):
                pe.wait_ge(o_ready, half + 1)
                nc.tensor.transpose(ps[:, 3, half * T:(half + 1) * T], o1f[:, half * P:(half + 1) * P],
                                    ident).then_inc(oT_ready, 1)

            for g in range(0, CHUNKS + 2, 2):
                if g == CHUNKS - 6:
                    pe.wait_ge(piece_max, NPIECE)
                    pe.wait_ge(acc_kept, 1)
                    sum_keys(0, 4).then_inc(z_ready, 1)
                if g == CHUNKS - 4:
                    turn_heads(0)
                if g == CHUNKS - 2:
                    pe.wait_ge(acc_kept, 2)
                    sum_keys(4, 7)
                a = 6 + g // 2
                if a < NPIECE:
                    max_piece(a)
                if g < CHUNKS:
                    score(g)
                    score(g + 1)
                if g >= 2:
                    weigh(g - 2)
                    weigh(g - 1)
                if g % 8 == 4 and g // 8 + 1 < PAIRS:
                    turn_max(g // 8 + 1)
            keep_clock(2, 6)
            pe.wait_ge(acc_kept, 3)
            sum_keys(7, 8).then_inc(z_ready, 1)
            keep_clock(4, 6)
            turn_heads(1)
            keep_clock(4, 6)
            pe.wait_ge(w_split, 1)
            pe.wait_ge(oT_kept, 2)
            pe.wait_ge(oT_rest, 2)
            project_split(ps[:, 2, 0:C], oT_hi, oT_lo, wo_hi, wo_lo, slice(0, C)).then_inc(wo_done, 1)
            keep_clock(12)
            pe.wait_ge(xn_ready, 2)
            turn(3, x1n).then_inc(xT_ready, 1)
            keep_clock(5)
            pe.wait_ge(w_split, 2)
            pe.wait_ge(xT_kept, 2)
            pe.wait_ge(x1T_rest, 1)
            for n, bank in enumerate((4, 5, 1)):
                project_split(ps[:, bank, 0:C], x1T_hi, x1T_lo, wqkv_hi, wqkv_lo,
                              slice(n * C, (n + 1) * C)).then_inc(qkv_done, 1)
            keep_clock(3)
            for half in range(2):
                if half == 0:
                    parts = [(dve_part, 1, 0), (pool_part, 1, 5), (dve_part, 2, 1), (pool_part, 2, 6), (pool_part, 3, 7),
                             (dve_part, 3, 3)]
                else:
                    parts = [(dve_part, 4, 0), (pool_part, 4, 5), (dve_part, 5, 1), (pool_part, 5, 6), (dve_part, 6, 3)]
                for n, (who, count, buf) in enumerate(parts):
                    pe.wait_ge(who, count)
                    last = nc.tensor.matmul(ps[:, 6 + half, :], ident, prod[buf][:, half * BANK:(half + 1) * BANK],
                                            start=(n == 0), stop=(n == len(parts) - 1))
                last.then_inc(s_done, 1)
            keep_clock(29)
            pieces = [(pv_dve, 1, prod[0], 4), (pv_dve, 2, prod[1], 4), (pv_pool, 1, pv_pool_prod[0], 2),
                      (pv_dve, 3, prod[2], 2)]
            total = sum(k for *_, k in pieces)
            n = 0
            for who, count, buf, k in pieces:
                pe.wait_ge(who, count)
                for i in range(k):
                    last = nc.tensor.matmul(ps[:, 0, 0:C], ident, buf[:, i * C:(i + 1) * C],
                                            start=(n == 0), stop=(n == total - 1))
                    n += 1
            last.then_inc(pv_done, 1)
            keep_clock(10, 3)
            pe.wait_ge(o_ready, 3)
            turn(1, o1f).then_inc(oT_ready, 1)
            keep_clock(5, 3)
            pe.wait_ge(w_split, 3)
            pe.wait_ge(oT_kept, 3)
            pe.wait_ge(oT_rest, 3)
            project_split(ps[:, 2, 0:C], oT_hi, oT_lo, wo2_hi, wo2_lo, slice(0, C)).then_inc(wo_done, 1)
            keep_clock(11)
            pe.wait_ge(xn_ready, 3)
            turn(3, x2n).then_inc(xT_ready, 1)
            keep_clock(5)
            pe.wait_ge(xT_kept, 3)
            pe.wait_ge(x2T_rest, 1)
            pe.wait_ge(ld["small"], 48)
            for n, part in enumerate((x2T_hi, x2T_lo)):
                for kc in range(KC):
                    last = nc.tensor.matmul(ps[:, 1, 0:E], part[:, kc, :].bitcast(F32), wr_s[:, kc, :],
                                            start=(n == 0 and kc == 0), stop=(n == 1 and kc == KC - 1))
            last.then_inc(logit_done, 1)

            def gate_up(e):
                pe.wait_ge(gu_hi_done, KC * e + KC)
                pe.wait_ge(gu_lo_pool, e + 1)
                pe.wait_ge(gu_lo_dve, 2 * (e + 1))
                if e >= 2:
                    pe.wait_ge(h_done, e - 1)
                for half in range(2):
                    last = project_split(ps[:, 4 + 2 * half + e % 2, :], x2T_hi, x2T_lo, gu_hi[e % 3], gu_lo[e],
                                         slice(half * I, (half + 1) * I))
                last.then_inc(gu_done, 1)

            def turn_hidden(e):
                pe.wait_ge(h_done, e + 1)
                if e >= 2:
                    pe.wait_ge(h_lo_done, e - 1)
                for ic in range(IC):
                    last = nc.tensor.transpose(ps[:, 2 + e % 2, ic * T:(ic + 1) * T], th[:, e % 2, ic * P:(ic + 1) * P],
                                               ident)
                last.then_inc(h_turned, 1)

            def down(e, first=0, end=3):
                for n, (a, b) in enumerate(((h_hi, dn_hi), (h_hi, dn_lo), (h_lo, dn_hi))):
                    if not first <= n < end:
                        continue
                    if n == 0:
                        pe.wait_ge(h_hi_done, e + 1)
                        pe.wait_ge(dn_hi_done, e + 1)
                    if n == 1:
                        pe.wait_ge(dn_lo_done, e + 1)
                    if n == 2:
                        pe.wait_ge(h_lo_done, e + 1)
                    for ic in range(IC):
                        last = nc.tensor.matmul(ps[:, 0, 0:C], a[:, e % 2, ic * T:(ic + 1) * T], b[e][:, ic, :],
                                                start=(e == 0 and n == 0 and ic == 0),
                                                stop=(e == E - 1 and n == 2 and ic == IC - 1))
                if end == 3:
                    last.then_inc(y_done, 1)

            gate_up(0)
            for e in range(E - 1):
                gate_up(e + 1)
                turn_hidden(e)
                if e >= 1:
                    down(e - 1)
            down(E - 2, end=2)
            turn_hidden(E - 1)
            down(E - 2, first=2)
            down(E - 1)

        @block.vector
        def _(dve):
            chain = [0]

            def link(ins):
                chain[0] += 1
                ins.then_inc(vchain, 1)
                dve.wait_ge(vchain, chain[0])

            dve.wait_ge(ld["wk"], 16)
            nc.vector.tensor_copy(wk_hi[:], wk_s[:]).then_inc(wk_split, 1)
            dve.wait_ge(wk_split, 1)
            nc.vector.tensor_tensor(wk_lo[:], wk_s[:], wk_hi[:].bitcast(F32), ALU.subtract).then_inc(wk_split, 1)

            def context_rest(i):
                sl = slice(i * BANK, (i + 1) * BANK)
                for kc in range(KC):
                    dve.wait_ge(ctx_hi_done, KC * i + kc + 1)
                    nc.vector.tensor_tensor(ctx_lo[:, kc, sl], ctx_raw[:, kc, sl], ctx_hi[:, kc, sl].bitcast(F32),
                                            ALU.subtract).then_inc(ctx_lo_done, 1)

            def key_rest(i):
                m, ch = divmod(i, KCH)
                dve.wait_ge(k_hi_done, i + 1)
                sl = slice(ch * BANK, (ch + 1) * BANK)
                nc.vector.tensor_tensor(k_lo[:, m, sl], ps[:, i % 4, :], k_hi[:, m, sl].bitcast(F32),
                                        ALU.subtract).then_inc(k_lo_done, 1)

            def moments(n, src):
                link(nc.vector.bn_stats(stat[:, n, :], src))
                nc.vector.bn_aggr(mv[:, n, :], stat[:, n, :]).then_inc(var_ready, 1)

            context_rest(0)
            context_rest(1)
            context_rest(2)
            key_rest(0)
            dve.wait_ge(ld["x"], 16)
            moments(0, xs[:])
            context_rest(3)
            dve.wait_ge(rstd_ready, 1)
            dve.wait_ge(var_ready, 1)
            link(nc.vector.tensor_scalar(hn[:], xs[:], mv[:, 0, 0:1], rstd[:, 0:1], ALU.subtract, ALU.mult))
            nc.vector.tensor_tensor_reduce(out=junk[:], in0=hn[:], in1=hn[:], scale=1.0 / C, scalar=0.0,
                                           op0=ALU.mult, op1=ALU.add, accum_out=ms[:, 0:1]).then_inc(var_ready, 1)
            key_rest(1)
            dve.wait_ge(rstd_ready, 2)
            nc.vector.tensor_scalar(h2[:], hn[:], rstd[:, 0:1], None, ALU.mult).then_inc(xn_ready, 1)
            for i in range(2, 5):
                key_rest(i)
            dve.wait_ge(xT_ready, 1)
            dve.wait_ge(ld["nw"], 16)
            for kc in range(KC):
                last = nc.vector.tensor_scalar(xnT[:, kc, :], ps[:, 7, kc * T:(kc + 1) * T], nw[:, kc:kc + 1], None,
                                               ALU.mult)
                link(last)
            nc.vector.engine_nop().then_inc(xT_kept, 1)
            key_rest(5)
            key_rest(6)

            def query_stacks(half):
                dve.wait_ge(q_turned, half + 1)
                pairs = slice(4 * half, 4 * half + 4)
                qp = ps[0:ROWS, 6 + half, :].rearrange("r (p t) -> r p t", t=T)
                for j in range(2):
                    nc.vector.tensor_scalar(qneg[0:ROWS, j, pairs], qp, cs[0:ROWS, C_S0 + j:C_S0 + j + 1], None,
                                            ALU.mult).then_inc(vchain, 1)
                chain[0] += 2
                dve.wait_ge(vchain, chain[0])
                for j in range(2):
                    nc.vector.scalar_tensor_tensor(qstack[0:ROWS, pairs, j, :], qp, cs[0:ROWS, C_M0 + j:C_M0 + j + 1],
                                                   qneg[0:ROWS, j, pairs].bitcast(F32), ALU.mult,
                                                   ALU.add).then_inc(q_kept, 1)

            key_rest(7)
            query_stacks(0)
            query_stacks(1)

            def reduce_piece(a):
                dve.wait_ge(piece, a + 1)
                nc.vector.tensor_reduce(part_max[:, a:a + 1], ps[:, 2 * (a % 2):2 * (a % 2) + 2, :], AX.XY,
                                        ALU.max).then_inc(piece_max, 1)
                if a % 2 == 1:
                    dve.wait_ge(piece_max, a + 1)
                    nc.vector.tensor_scalar(row_max[:, a // 2:a // 2 + 1], part_max[:, a - 1:a], part_max[:, a:a + 1],
                                            FLOOR, ALU.max, ALU.max).then_inc(rowmax, 1)

            def normalise(half):
                hs = slice(8 * half, 8 * half + 8)
                dve.wait_ge(z_ready, half + 1)
                z = ps[:, half, 0:C].rearrange("p (h w) -> p h w", h=8)
                link(nc.vector.tensor_scalar(den[:, hs], z[:, :, HD], 1e-30, None, ALU.max))
                link(nc.vector.reciprocal(rden[:, hs], den[:, hs]))
                nc.vector.tensor_tensor(o1[:, hs, :], z[:, :, 0:HD], rden[:, hs].unsqueeze(2).broadcast_to([P, 8, HD]),
                                        ALU.mult).then_inc(o_ready, 1)

            def keep_rest(half):
                dve.wait_ge(oT_kept, half + 1)
                nc.vector.tensor_tensor(oT_lo[:, half, :], ps[:, 3, half * T:(half + 1) * T],
                                        oT_hi[:, half, :].bitcast(F32), ALU.subtract).then_inc(oT_rest, 1)

            for a in range(NPIECE):
                reduce_piece(a)
                if a == 23:
                    dve.wait_ge(weighed, CHUNKS // 2)
                    nc.vector.tensor_copy(acc_s[:, 0:4, :], ps[:, 6, :].rearrange("p (c t) -> p c t", c=4)).then_inc(acc_kept, 1)
            dve.wait_ge(g_kept, 1)
            link(nc.vector.tensor_scalar(gate[:], gate[:], 0.5, 0.5, ALU.mult, ALU.add))
            dve.wait_ge(ld["small"], 48)
            for n in range(2):
                nc.vector.tensor_tensor_reduce(out=junk[:, n * D2:(n + 1) * D2], in0=lam_s[:, 2 * n, :],
                                               in1=lam_s[:, 2 * n + 1, :], scale=1.0, scalar=0.0, op0=ALU.mult,
                                               op1=ALU.add, accum_out=lsum[:, n:n + 1]).then_inc(lam_in, 1)
            dve.wait_ge(weighed, CHUNKS - 8)
            nc.vector.tensor_copy(acc_s[:, 4:7, :], ps[:, 7, 0:3 * T].rearrange("p (c t) -> p c t", c=3)).then_inc(acc_kept, 1)
            normalise(0)
            keep_rest(0)
            dve.wait_ge(weighed, CHUNKS)
            nc.vector.tensor_copy(acc_s[:, 7, :], ps[:, 2, 0:T]).then_inc(acc_kept, 1)
            dve.wait_ge(lam_exp, 1)
            link(nc.vector.tensor_scalar(nlam[:], lexp[:, 1:2], lexp[:, 0:1], LAM_INIT, ALU.subtract, ALU.subtract))
            normalise(1)
            keep_rest(1)
            dve.wait_ge(wo_done, 1)
            link(nc.vector.tensor_tensor(junk[:], ps[:, 2, 0:C], gate[:], ALU.mult))
            link(nc.vector.tensor_tensor(x1[:], junk[:], xs[:], ALU.add))
            moments(1, x1[:])

            def rest(lo, hi, bank, kept, count, done):
                dve.wait_ge(kept, count)
                nc.vector.tensor_tensor(lo[:], ps[:, bank, 0:C].rearrange("p (c t) -> p c t", c=KC),
                                        hi[:].bitcast(F32), ALU.subtract).then_inc(done, 1)

            nc.vector.tensor_tensor(x1b[:], x1[:], bo_s[:], ALU.add).then_inc(vchain, 1)
            chain[0] += 1
            dve.wait_ge(rstd_ready, 3)
            dve.wait_ge(var_ready, 3)
            nc.vector.tensor_scalar(x1n[:], x1[:], mv[:, 1, 0:1], rstd[:, 1:2], ALU.subtract, ALU.mult).then_inc(xn_ready, 1)
            rest(x1T_lo, x1T_hi, 3, xT_kept, 2, x1T_rest)
            dve.wait_ge(qkv_done, 2)
            nc.vector.tensor_copy(kd[:], ps[:, 5, 0:C].rearrange("p (d s) -> p d s", d=D2)).then_inc(k2_kept, 1)
            dve.wait_ge(k2_kept, 1)
            dve.wait_ge(q2_kept, 1)

            def product(half, d):
                rows = slice(half * NH, (half + 1) * NH)
                return nc.vector.tensor_tensor(prod[d][:, half * BANK:(half + 1) * BANK].rearrange("p (a b) -> p a b", a=NH),
                                               qd[:, d, rows].unsqueeze(2).broadcast_to([P, NH, SUB]),
                                               kd[:, d, :].unsqueeze(1).broadcast_to([P, NH, SUB]), ALU.mult)

            def scores_products(half):
                cols = slice(half * BANK, (half + 1) * BANK)
                product(half, 0).then_inc(dve_part, 1)
                for b in (1, 3):
                    product(half, b).then_inc(vchain, 1)
                    product(half, b + 1).then_inc(vchain, 1)
                    chain[0] += 2
                    dve.wait_ge(vchain, chain[0])
                    nc.vector.tensor_tensor(prod[b][:, cols], prod[b][:, cols], prod[b + 1][:, cols],
                                            ALU.add).then_inc(dve_part, 1)

            def softmax_shift(half):
                rows = slice(half * NH, (half + 1) * NH)
                sc = ps[:, 6 + half, :].rearrange("p (a k) -> p a k", k=SUB)
                dve.wait_ge(s_done, half + 1)
                link(nc.vector.tensor_reduce(smax[:, rows], sc, AX.X, ALU.max))
                link(nc.vector.tensor_scalar(smax[:, rows], smax[:, rows], FMAX, -FMAX, ALU.min, ALU.max))
                nc.vector.scalar_tensor_tensor(shifted[:, rows, :], sc, FMAX,
                                               smax[:, rows].unsqueeze(2).broadcast_to([P, NH, SUB]),
                                               ALU.min, ALU.subtract).then_inc(shifted_ready, 1)

            scores_products(0)
            scores_products(1)
            softmax_shift(0)
            softmax_shift(1)
            for half in range(2):
                rows = slice(half * NH, (half + 1) * NH)
                dve.wait_ge(sexp, half + 1)
                nc.vector.tensor_reduce(ssum[:, rows], shifted[:, rows, :], AX.X, ALU.add).then_inc(vchain, 1)
            chain[0] += 2
            dve.wait_ge(vchain, chain[0])
            link(nc.vector.reciprocal(srec[:], ssum[:]))
            nc.vector.tensor_tensor(dif[:], shifted[:, 0:NH, 0:NH],
                                    srec[:, 0:NH].unsqueeze(2).broadcast_to([P, NH, NH]), ALU.mult).then_inc(vchain, 1)
            chain[0] += 1
            link(nc.vector.scalar_tensor_tensor(dif1[:], shifted[:, NH:SUB, NH:SUB], nlam[:, 0:1],
                                                srec[:, NH:SUB].unsqueeze(2).broadcast_to([P, NH, NH]),
                                                ALU.mult, ALU.mult))
            nc.vector.tensor_tensor(dif[:], dif[:], dif1[:], ALU.add).then_inc(dif_ready, 1)
            dve.wait_ge(dif_ready, 1)
            dve.wait_ge(v2_kept, 1)

            def weighted(buf, h0, n):
                return nc.vector.tensor_tensor(
                    prod[buf][:, 0:n * C].rearrange("p (h a d) -> p h a d", h=n, a=NH),
                    dif[:, :, h0:h0 + n].rearrange("p a h -> p h a").unsqueeze(3).broadcast_to([P, n, NH, HD]),
                    vd[:, h0:h0 + n, :].unsqueeze(2).broadcast_to([P, n, NH, HD]), ALU.mult)

            weighted(0, 0, 4).then_inc(pv_dve, 1)
            weighted(1, 4, 4).then_inc(pv_dve, 1)
            link(weighted(2, 8, 2))
            link(weighted(3, 10, 2))
            nc.vector.tensor_tensor(prod[2][:, 0:2 * C], prod[2][:, 0:2 * C], prod[3][:, 0:2 * C], ALU.add).then_inc(pv_dve, 1)

            def gate_up_lo(e, kc):
                cols = slice(0, 2 * I if kc == 0 else GU_SPLIT)
                dve.wait_ge(gu_hi_done, KC * e + kc + 1)
                nc.vector.tensor_tensor(gu_lo[e][:, kc, cols], gu_w[e][:, kc, cols],
                                        gu_hi[e % 3][:, kc, cols].bitcast(F32), ALU.subtract).then_inc(gu_lo_dve, 1)

            gate_up_lo(0, 0)
            gate_up_lo(0, 1)
            gate_up_lo(1, 0)
            dve.wait_ge(sq_done, 1)
            nc.vector.tensor_reduce(ssq[:], sq[:], AX.X, ALU.add).then_inc(var_ready, 1)
            dve.wait_ge(root_kept, 1)
            link(nc.vector.reciprocal(rms[:], rms[:]))
            nc.vector.tensor_tensor(o1[:], ps[:, 0, 0:C].rearrange("p (h d) -> p h d", h=NH),
                                    rms[:].unsqueeze(2).broadcast_to([P, NH, HD]), ALU.mult).then_inc(o_ready, 1)
            gate_up_lo(1, 1)
            rest(oT_lo, oT_hi, 1, oT_kept, 3, oT_rest)
            dve.wait_ge(wo_done, 2)
            link(nc.vector.tensor_tensor(x2[:], ps[:, 2, 0:C], x1b[:], ALU.add))
            moments(2, x2[:])
            dve.wait_ge(rstd_ready, 4)
            dve.wait_ge(var_ready, 5)
            nc.vector.tensor_scalar(x2n[:], x2[:], mv[:, 2, 0:1], rstd[:, 2:3], ALU.subtract, ALU.mult).then_inc(xn_ready, 1)
            rest(x2T_lo, x2T_hi, 3, xT_kept, 3, x2T_rest)
            gate_up_lo(2, 0)
            dve.wait_ge(logit_done, 1)
            link(nc.vector.tensor_copy(lg[:], ps[:, 1, 0:E]))
            link(nc.vector.tensor_reduce(lmax[:], lg[:], AX.X, ALU.max))
            nc.vector.tensor_scalar(lex[:], lg[:], lmax[:, 0:1], None, ALU.subtract).then_inc(lg_ready, 1)
            mine, other = lg[:].unsqueeze(2).broadcast_to([P, E, E]), lg[:].unsqueeze(1).broadcast_to([P, E, E])
            link(nc.vector.tensor_tensor(rk[:], other, mine, ALU.is_gt))
            link(nc.vector.tensor_tensor(rk2[:], other, mine, ALU.is_equal))
            link(nc.vector.tensor_tensor(rk2[:], rk2[:], cs[:, C_TRI:C_ALL].rearrange("p (i j) -> p i j", i=E), ALU.mult))
            link(nc.vector.tensor_tensor(rk[:], rk[:], rk2[:], ALU.add))
            link(nc.vector.tensor_reduce(rank[:], rk[:], AX.X, ALU.add))
            dve.wait_ge(lex_done, 1)
            link(nc.vector.scalar_tensor_tensor(wsel[:], rank[:], 2.0, lex[:], ALU.is_lt, ALU.mult))
            link(nc.vector.tensor_reduce(wsum[:, 0:1], wsel[:], AX.X, ALU.add))
            link(nc.vector.reciprocal(wsum[:, 1:2], wsum[:, 0:1]))
            link(nc.vector.tensor_scalar(wsel[:], wsel[:], wsum[:, 1:2], 0.5, ALU.mult, ALU.mult))

            def hidden(e):
                own = th[:, e % 2, :]
                dve.wait_ge(th_done, e + 1)
                link(nc.vector.scalar_tensor_tensor(own, own, 1.0, ps[:, 4 + e % 2, :], ALU.add, ALU.mult))
                nc.vector.scalar_tensor_tensor(own, own, wsel[:, e:e + 1], ps[:, 6 + e % 2, :], ALU.mult,
                                               ALU.mult).then_inc(h_done, 1)

            def hidden_lo(e):
                dve.wait_ge(h_hi_done, e + 1)
                nc.vector.tensor_tensor(h_lo[:, e % 2, :], ps[:, 2 + e % 2, :], h_hi[:, e % 2, :].bitcast(F32),
                                        ALU.subtract).then_inc(h_lo_done, 1)

            gate_up_lo(2, 1)
            hidden(0)
            for e in range(E):
                if e + 1 < E:
                    hidden(e + 1)
                hidden_lo(e)
                if e + 3 < E:
                    gate_up_lo(e + 3, 0)
                    gate_up_lo(e + 3, 1)
            dve.wait_ge(y_done, E)
            nc.vector.tensor_tensor(x2[:], x2[:], ps[:, 0, 0:C], ALU.add).then_inc(out_ready, 1)


def _turned(w, rows=slice(None)):
    w = np.asarray(w)[rows]
    return np.ascontiguousarray(w.T.reshape(-1, P, w.shape[0]).transpose(1, 0, 2))


def kernel(**inputs):
    import concourse.bacc as _bacc
    from concourse.bass_utils import run_bass_kernel_spmd as _run

    a = {k: np.asarray(v) for k, v in inputs.items()}
    sub = np.arange(C).reshape(NH, D2, 2).transpose(1, 2, 0).reshape(-1)
    wqkv = np.concatenate([_turned(a["L0_attn_Wq"], sub), _turned(a["L0_attn_Wk"], sub), _turned(a["L0_attn_Wv"])], axis=2)
    lams = np.stack([a["L0_attn_lq1"], a["L0_attn_lk1"], a["L0_attn_lq2"], a["L0_attn_lk2"]])
    gu = a["L0_ffn_gate_up_proj"]
    dn = a["L0_ffn_down_proj"]
    arrays = {
        "x": a["x"][0],
        "ctxT": _turned(a["ctx_2048"][0]),
        "mask2": np.broadcast_to(a["mask_BxS2_bk0"], (2, S)),
        "cst": constants(),
        "norm_w": a["L0_xattn_norm_w"].reshape(KC, P).T,
        "wk": _turned(a["L0_xattn_wk"]),
        "wv": _turned(a["L0_xattn_wv"]),
        "wqg": np.concatenate([_turned(a["L0_xattn_wq"]), _turned(a["L0_xattn_wg"])], axis=2),
        "wo": _turned(a["L0_xattn_wo"]),
        "wqkv": wqkv,
        "wo2": _turned(a["L0_attn_Wo"]),
        "bo": np.broadcast_to(a["L0_attn_bo"], (P, C)),
        "lams": np.broadcast_to(lams, (P, 4, D2)),
        "wr": _turned(a["L0_ffn_gate_weight"]),
        "wgu": np.stack([_turned(gu[e]) for e in range(E)]),
        "wdn": np.stack([_turned(dn[e]) for e in range(E)]),
    }
    nc = _bacc.Bacc("TRN2", target_bir_lowering=False, num_devices=1)
    feed, args = {}, []
    for name, v in arrays.items():
        v = np.ascontiguousarray(v)
        feed[f"in_{name}"] = v
        args.append(nc.dram_tensor(f"in_{name}", v.shape, mybir.dt.from_np(v.dtype), kind="ExternalInput").ap())
    out = nc.dram_tensor("out_0", (T, C), F32, kind="ExternalOutput").ap()
    perceiver_layer(nc, *args, out)
    r = _run(nc, [feed], core_ids=[0])
    return r.results[0]["out_0"].reshape(1, T, C)
```
